# Optimizing a Trainium2 kernel written in Bass

```python
import numpy as np
import jax
import jax.numpy as jnp

def _softmax(x, axis=-1):
    return jax.nn.softmax(x, axis=axis)

def _gelu(x):
    return jax.nn.gelu(x, approximate=True)

def _silu(x):
    return jax.nn.silu(x)

def _sigmoid(x):
    return jax.nn.sigmoid(x)

def _layernorm(x, axis=-1, eps=1e-05):
    m = jnp.mean(x, axis=axis, keepdims=True)
    v = jnp.var(x, axis=axis, keepdims=True)
    return (x - m) / jnp.sqrt(v + eps)

def _scatter_add(tgt, idx, src, axis=0):
    return tgt.at[idx].add(src)

def _segment_sum(src, seg, n):
    return jax.ops.segment_sum(src, seg, n)
kernel_name = 'mk_gnn_preln_d2_gnn_r64_6a6c5a'

def setup_inputs(seed: int=0):
    np.random.seed(seed)
    _w = jnp.asarray

    def _rec_inputs():
        import jax
        import jax.numpy as jnp
        _gk = jax.random.key(seed)
        x = -0.0007083 + 1.001 * jax.random.normal(jax.random.fold_in(_gk, 1), (100000, 48), jnp.float32)
        src = jax.random.randint(jax.random.fold_in(_gk, 2), (25000,), 0, 100000, jnp.int32)
        dst = jnp.minimum((100000 * jax.random.uniform(jax.random.fold_in(_gk, 3), (25000,)) ** 2.0).astype(jnp.int32), 99999)
        _o = jnp.argsort(dst, stable=True)
        src = src[_o]
        dst = dst[_o]
        edge_attr_40 = jax.random.uniform(jax.random.fold_in(_gk, 13), (25000, 40), jnp.float32, 0.0, 1)
        edge_type_8 = jax.random.randint(jax.random.fold_in(_gk, 15), (25000,), 0, 8, jnp.int32)
        edge_weight = jax.random.uniform(jax.random.fold_in(_gk, 16), (25000,), jnp.float32, 0.0, 6.99999)
        edge_weight1 = jax.random.uniform(jax.random.fold_in(_gk, 17), (25000, 1), jnp.float32, 0.0, 1)
        node_type_119 = jax.random.randint(jax.random.fold_in(_gk, 18), (100000,), 0, 119, jnp.int32)
        node_vec = jax.random.uniform(jax.random.fold_in(_gk, 19), (100000,), jnp.float32, 0.0, 1.49999)
        return (x, src, dst, edge_attr_40, edge_type_8, edge_weight, edge_weight1, node_type_119, node_vec)
    x, src, dst, edge_attr_40, edge_type_8, edge_weight, edge_weight1, node_type_119, node_vec = _rec_inputs()

    def _L0_gnn_setup():
        import jax, jax.numpy as jnp
        import numpy as np
        CUTOFF = 6.0
        LN_EPS = 1e-05
        key = jax.random.key(seed)
        ks = jax.random.split(key, 16)
        N, E, H, R, NEL, G = (50000, 12500, 48, 40, 119, 32)
        inp = {'h': jax.random.normal(ks[0], (N, H), jnp.float32), 'edge_index': jax.random.randint(ks[1], (2, E), 0, N, jnp.int64), 'edge_attr': jax.random.uniform(ks[2], (E, R), jnp.float32), 'distances': jax.random.uniform(ks[3], (E,), jnp.float32) * 7.0, 'atom_z': jax.random.randint(ks[4], (N,), 0, NEL, jnp.int64), 'node_mult': jax.random.uniform(ks[5], (N,), jnp.float32) + 0.5, 'batch': jnp.zeros((N,), jnp.int64), 'W1': jax.random.normal(ks[6], (H, R), jnp.float32) / np.sqrt(R), 'b1': jax.random.normal(ks[7], (H,), jnp.float32) * 0.01, 'W2': jax.random.normal(ks[8], (H, H), jnp.float32) / np.sqrt(H), 'b2': jax.random.normal(ks[9], (H,), jnp.float32) * 0.01, 'emb': jax.random.normal(ks[10], (NEL, G), jnp.float32) * 0.01, 'adaptW': jax.random.normal(ks[11], (G, G), jnp.float32) * 0.01, 'gamma': jnp.ones((H,), jnp.float32), 'beta': jnp.zeros((H,), jnp.float32)}
        return inp
    _L0_gnn_all = _L0_gnn_setup()
    _L0_gnn_in = {k: v for k, v in _L0_gnn_all.items() if k in ('W1', 'b1', 'W2', 'b2', 'emb', 'adaptW', 'gamma', 'beta')}
    del _L0_gnn_all

    def _L1_gnn_setup():
        import jax, jax.numpy as jnp
        import numpy as np
        N_NODES = 50000
        N_EDGES = 25000
        IN_FEAT = 48
        OUT_FEAT = 48
        NUM_RELS = 8
        key = jax.random.key(seed)
        ks = jax.random.split(key, 9)
        s1 = float(np.sqrt(2.0) * np.sqrt(6.0 / (IN_FEAT + IN_FEAT)))
        s2 = float(np.sqrt(2.0) * np.sqrt(6.0 / (IN_FEAT + OUT_FEAT)))
        return {'inputs': jax.random.normal(ks[0], (N_NODES, IN_FEAT), dtype=jnp.float32), 'norm': jax.random.uniform(ks[1], (N_EDGES, 1), dtype=jnp.float32), 'weight1': jax.random.uniform(ks[2], (NUM_RELS, IN_FEAT, IN_FEAT), jnp.float32, -s1, s1), 'weight2': jax.random.uniform(ks[3], (NUM_RELS, IN_FEAT, OUT_FEAT), jnp.float32, -s2, s2), 'bias1': jax.random.normal(ks[4], (IN_FEAT,), dtype=jnp.float32) * 0.1, 'bias2': jax.random.normal(ks[5], (OUT_FEAT,), dtype=jnp.float32) * 0.1, 'src': jax.random.randint(ks[6], (N_EDGES,), 0, N_NODES, dtype=jnp.int64) if jax.config.jax_enable_x64 else jax.random.randint(ks[6], (N_EDGES,), 0, N_NODES).astype(jnp.int32), 'dst': jax.random.randint(ks[7], (N_EDGES,), 0, N_NODES).astype(jnp.int32), 'rel_type': jax.random.randint(ks[8], (N_EDGES,), 0, NUM_RELS).astype(jnp.int32)}
    _L1_gnn_all = _L1_gnn_setup()
    _L1_gnn_in = {k: v for k, v in _L1_gnn_all.items() if k in ('weight1', 'weight2', 'bias1', 'bias2')}
    del _L1_gnn_all
    return {'x': x, 'src': src, 'dst': dst, 'edge_attr_40': edge_attr_40, 'edge_type_8': edge_type_8, 'edge_weight': edge_weight, 'edge_weight1': edge_weight1, 'node_type_119': node_type_119, 'node_vec': node_vec, 'L0_gnn_W1': _L0_gnn_in['W1'], 'L0_gnn_b1': _L0_gnn_in['b1'], 'L0_gnn_W2': _L0_gnn_in['W2'], 'L0_gnn_b2': _L0_gnn_in['b2'], 'L0_gnn_emb': _L0_gnn_in['emb'], 'L0_gnn_adaptW': _L0_gnn_in['adaptW'], 'L0_gnn_gamma': _L0_gnn_in['gamma'], 'L0_gnn_beta': _L0_gnn_in['beta'], 'L1_gnn_weight1': _L1_gnn_in['weight1'], 'L1_gnn_weight2': _L1_gnn_in['weight2'], 'L1_gnn_bias1': _L1_gnn_in['bias1'], 'L1_gnn_bias2': _L1_gnn_in['bias2']}

def reference(x, src, dst, edge_attr_40, edge_type_8, edge_weight, edge_weight1, node_type_119, node_vec, L0_gnn_W1, L0_gnn_b1, L0_gnn_W2, L0_gnn_b2, L0_gnn_emb, L0_gnn_adaptW, L0_gnn_gamma, L0_gnn_beta, L1_gnn_weight1, L1_gnn_weight2, L1_gnn_bias1, L1_gnn_bias2):
    import jax
    import jax.numpy as jnp

    def _L0_gnn_ref(h, edge_index, edge_attr, distances, atom_z, node_mult, batch, W1, b1, W2, b2, emb, adaptW, gamma, beta):
        import jax, jax.numpy as jnp
        import numpy as np
        CUTOFF = 6.0
        LN_EPS = 1e-05
        src, dst = (edge_index[0], edge_index[1])
        N = h.shape[0]
        gate = jax.nn.silu(edge_attr @ W1.T + b1) @ W2.T + b2
        ei = emb[atom_z[src]]
        ej = emb[atom_z[dst]]
        adapt_logit = jnp.sum(ei * (ej @ adaptW.T), axis=-1, keepdims=True)
        gate = gate + adapt_logit
        cw = jnp.where(distances < CUTOFF, 0.5 * (jnp.cos(jnp.pi * distances / CUTOFF) + 1.0), 0.0)
        mj = node_mult[dst]
        msg = gate * h[dst] * (cw * mj)[:, None]
        agg = jax.ops.segment_sum(msg, src, num_segments=N)
        tot = jax.ops.segment_sum(mj, src, num_segments=N)
        agg = agg / jnp.clip(tot, 1e-08, None)[:, None]
        x = h + agg
        mu = jnp.mean(x, axis=-1, keepdims=True)
        var = jnp.mean(jnp.square(x - mu), axis=-1, keepdims=True)
        return (x - mu) / jnp.sqrt(var + LN_EPS) * gamma + beta

    def _L1_gnn_ref(inputs, norm, weight1, weight2, bias1, bias2, src, dst, rel_type):
        import jax, jax.numpy as jnp
        import numpy as np
        N_NODES = 50000
        N_EDGES = 25000
        IN_FEAT = 48
        OUT_FEAT = 48
        NUM_RELS = 8
        h1 = jax.nn.relu(jnp.einsum('ni,rij->nrj', inputs, weight1) + bias1)
        h2 = jnp.einsum('nrj,rjo->nro', h1, weight2)
        msg = h2[src, rel_type] * norm
        agg = jax.ops.segment_sum(msg, dst, num_segments=inputs.shape[0])
        return jax.nn.relu(agg + bias2)
    edge_index = jnp.stack([src, dst])
    batch0 = jnp.zeros((100000,), jnp.int32)
    h = jnp.maximum(_layernorm(x, axis=-1), 0.0)
    x = x + _L0_gnn_ref(h, edge_index, edge_attr_40, edge_weight, node_type_119, node_vec, batch0, L0_gnn_W1, L0_gnn_b1, L0_gnn_W2, L0_gnn_b2, L0_gnn_emb, L0_gnn_adaptW, L0_gnn_gamma, L0_gnn_beta)
    h = jnp.maximum(_layernorm(x, axis=-1), 0.0)
    x = x + _L1_gnn_ref(h, edge_weight1, L1_gnn_weight1, L1_gnn_weight2, L1_gnn_bias1, L1_gnn_bias2, src, dst, edge_type_8)
    return x

_drawn_inputs = setup_inputs


def setup_inputs(seed=0):
    import zlib

    import numpy as np

    out = dict(_drawn_inputs(seed))
    spreads = {'L0_gnn_gamma': (1.0, 0.2), 'L0_gnn_beta': (0.0, 0.1)}
    factors = {'node_vec': 64.0,
     'L0_gnn_b1': 56.771,
     'L0_gnn_b2': 38.141,
     'L0_gnn_emb': 64.0,
     'L0_gnn_adaptW': 64.0,
     'L1_gnn_bias1': 5.931}
    for name, (base, spread) in spreads.items():
        noise = np.random.default_rng([zlib.crc32(name.encode()), seed]).standard_normal(out[name].shape)
        drawn = base * np.exp(spread * noise) if base else spread * noise
        out[name] = jnp.asarray(drawn.astype(out[name].dtype))
    for name, factor in factors.items():
        out[name] = (out[name] * factor).astype(out[name].dtype)
    return out
```

```python
from contextlib import ExitStack

import concourse.bass as bass
from concourse import mybir
import numpy as np

F32 = mybir.dt.float32
I32 = mybir.dt.int32
ALU = mybir.AluOpType
ACT = mybir.ActivationFunctionType
AX_X = mybir.AxisListType.X

P = 128
N = 100000
E = 25000
H = 48
RAD = 40
NREL = 8
NTYPE = 119
GEMB = 32
CUTOFF = 6.0
EPS = 1e-5

TILES = 4
BE = TILES * P
NBLOCK = -(-E // BE)
NR = 16
NP = NBLOCK * P * NR
NULL = N
DUMP = NP - 2 * P
assert NULL < DUMP and NP >= N
TW = H + 2
AW = H + 1
HW = 2 * H
G1 = 2 * TILES + NR
G2 = TILES + NR
CW1 = NREL * H
KC = CW1 // P
OFF = -1.0e30
ADDS = 16 * TILES
LOOPS = NBLOCK // 2
assert NBLOCK == 2 * LOOPS + 1 and CW1 == KC * P


def build(nc, table, edge_idx, edge_rows, edge_feat, dist, norm, rel, w1t, b1, w2b, embt, adaptt,
          gamma, beta, rw1, rb1, rw2, rb2, out):
    agg0 = nc.dram_tensor("agg0", [NP, AW], F32).ap()
    agg1 = nc.dram_tensor("agg1", [NP, H], F32).ap()
    kept = nc.dram_tensor("kept", [NBLOCK, P, G2 * HW], F32).ap()
    dst_once = nc.dram_tensor("dst_once", [NBLOCK, P, TILES], I32).ap()
    x_mid = nc.dram_tensor("x_mid", [NBLOCK, P, NR * H], F32).ap()
    table_chunks = table.rearrange("(c p r) w -> c p (r w)", p=P, r=NR)
    agg0_chunks = agg0.rearrange("(c p r) w -> c p (r w)", p=P, r=NR)
    agg1_chunks = agg1.rearrange("(c p r) w -> c p (r w)", p=P, r=NR)
    out_chunks = out.rearrange("(c p r) w -> c p (r w)", p=P, r=NR)

    with ExitStack() as ctx:
        def sb(name, shape, dt=F32):
            return ctx.enter_context(nc.sbuf_tensor(name, shape, dt))

        def sem(name):
            return ctx.enter_context(nc.semaphore(name))

        def pair_of(make, name, *args):
            return [make(f"{name}_{s}", *args) for s in range(2)]

        ident = sb("ident", [P, P])
        iota_type = sb("iota_type", [P, NTYPE])
        iota_rel = sb("iota_rel", [P, NREL])
        earlier = sb("earlier", [P, 2 * P])
        dump_id = sb("dump_id", [P, 2, TILES])
        zeros = sb("zeros", [P, NR * AW])
        bias_rows = sb("bias_rows", [P, NR, H])
        half_pi = sb("half_pi", [P, 1])
        eps = sb("eps", [P, 1])
        w1t_sb = sb("w1t_sb", [RAD, H])
        b1_sb = sb("b1_sb", [H, 1])
        w2b_sb = sb("w2b_sb", [H + 1, H])
        embt_sb = sb("embt_sb", [GEMB, NTYPE])
        adaptt_sb = sb("adaptt_sb", [GEMB, GEMB])
        ada = sb("ada", [GEMB, NTYPE])
        q_sb = sb("q_sb", [NTYPE, NTYPE])
        gamma_b = sb("gamma_b", [P, H])
        beta_b = sb("beta_b", [P, H])
        rb2_b = sb("rb2_b", [P, H])
        rw1_sb = sb("rw1_sb", [H + NREL, CW1])
        rw2_sb = sb("rw2_sb", [P, KC, H])
        dist_sb = sb("dist_sb", [P, NBLOCK * TILES])
        cw_a = sb("cw_a", [P, NBLOCK * TILES])
        cw_b = sb("cw_b", [P, NBLOCK * TILES])
        cw_all = sb("cw_all", [P, NBLOCK * TILES])

        idx = pair_of(sb, "idx", [P, 2 * TILES], I32)
        rows = pair_of(sb, "rows", [P, 2 * BE], I32)
        feat = pair_of(sb, "feat", [RAD, BE])
        nodes = pair_of(sb, "nodes", [P, G1, TW])
        once = pair_of(sb, "once", [P, 2 * TILES], I32)
        kept_out = pair_of(sb, "kept_out", [P, G2, HW])
        sums = pair_of(sb, "sums", [P, TILES, AW])
        stat = sb("stat", [P, G1])
        nmean = sb("nmean", [P, G1])
        cen = sb("cen", [P, G1, H])
        sq = sb("sq", [P, G1, H])
        var = sb("var", [P, G1])
        std = sb("std", [P, G1])
        rstd = sb("rstd", [P, G1])
        nrm = sb("nrm", [P, G1, H])
        hid = sb("hid", [P, G1, H])
        hsum = sb("hsum", [P, G2])
        hmean = sb("hmean", [P, G2])
        same_a = sb("same_a", [P, 2, P])
        same_b = sb("same_b", [P, 2, 2 * P])
        junk = sb("junk", [P, 2 * TILES, 2 * P])
        junk_q = sb("junk_q", [P, TILES, NTYPE])
        ahead = sb("ahead", [P, 2 * TILES])
        turn = sb("turn", [P, 2 * TILES])
        turned = sb("turned", [P, 2 * TILES])
        onehot = sb("onehot", [P, TILES, NTYPE])
        onehot_t = sb("onehot_t", [NTYPE, TILES, P])
        gate_in = sb("gate_in", [64, BE])
        logit = sb("logit", [P, TILES])
        coef = sb("coef", [P, TILES])
        hdst = sb("hdst", [P, TILES, H])
        msg_raw = sb("msg_raw", [P, TILES, H])
        msum = sb("msum", [P, TILES])
        mmean = sb("mmean", [P, TILES])
        msg = sb("msg", [P, TILES, AW])
        agg_in = pair_of(sb, "agg_in", [P, G2, AW])
        kept_in = pair_of(sb, "kept_in", [P, G2, HW])
        edge_sc = pair_of(sb, "edge_sc", [P, 2 * TILES])
        didx = pair_of(sb, "didx", [P, TILES], I32)
        x2 = pair_of(sb, "x2", [P, G2, H])
        sums1 = pair_of(sb, "sums1", [P, TILES, H])
        tot = sb("tot", [P, G2])
        rtot = sb("rtot", [P, G2])
        ycen = sb("ycen", [P, G2, H])
        ycen2 = sb("ycen2", [P, G2, H])
        ysq = sb("ysq", [P, G2, H])
        yvar = sb("yvar", [P, G2])
        ystd = sb("ystd", [P, G2])
        yrstd = sb("yrstd", [P, G2])
        ynrm = sb("ynrm", [P, G2, H])
        ygam = sb("ygam", [P, G2, H])
        h2 = sb("h2", [P, TILES, H + NREL])
        h2n = sb("h2n", [P, TILES, H])
        h2_t = sb("h2_t", [H + NREL, BE])
        hid1 = sb("hid1", [P, KC, BE])
        msg1 = sb("msg1", [P, TILES, H])
        agg_last = pair_of(sb, "agg_last", [P, NR * H])
        x_last = pair_of(sb, "x_last", [P, NR * H])
        out_sb = pair_of(sb, "out_sb", [P, NR * H])

        def psum(name, shape):
            return ctx.enter_context(nc.psum_tensor(name, shape, F32))

        ps_t = psum("ps_t", [P, 512])
        ps_q = psum("ps_q", [P, 512])
        ps_h = psum("ps_h", [P, 512])
        ps_m = psum("ps_m", [P, 512])
        ps_s = psum("ps_s", [P, 512])
        ps_k = [psum(f"ps_k{k}", [P, 512]) for k in range(KC)]

        consts_in = sem("consts_in")
        rw1_in = sem("rw1_in")
        rb1_in = sem("rb1_in")
        agg0_set = sem("agg0_set")
        agg1_set = sem("agg1_set")
        idx_in = pair_of(sem, "idx_in")
        feat_in = pair_of(sem, "feat_in")
        rows_in = pair_of(sem, "rows_in")
        chunk_in = pair_of(sem, "chunk_in")
        ends_in = pair_of(sem, "ends_in")
        added0 = pair_of(sem, "added0")
        kept_stored = pair_of(sem, "kept_stored")
        names1 = ("mean_done nmean_done cen_done sq_done var_done std_done rstd_done nrm_done hid_done "
                  "hsum_done hmean_done kept_done ahead_done turn_done turned_done once_done same_done "
                  "onehot_done onehot_t_done onehot_copied q_done logit_done h1_done gate_in_done gate_done "
                  "coef_done hdst_done raw_done mmean_done msg_done sums_done sums_copied").split()
        names2 = ("tot_done rtot_done ydiv_done ycen_done ysq_done yvar_done ystd_done yrstd_done ynrm_done "
                  "ygam_done x2_done esum_done emean_done ecen_done esq_done evar_done estd_done erstd_done "
                  "enrm_done h2_done rel_done h2t_done h2t_copied k1_done hid1_done m1_done msg1_done same1_done "
                  "sums1_done sums1_copied").split()
        S = {n: sem(n) for n in names1 + names2}
        agg_chunk_in = pair_of(sem, "agg_chunk_in")
        agg_ends_in = pair_of(sem, "agg_ends_in")
        kept_got = pair_of(sem, "kept_got")
        idx2_in = pair_of(sem, "idx2_in")
        rows2_in = pair_of(sem, "rows2_in")
        adds0_done = sem("adds0_done")
        adds1_done = sem("adds1_done")
        added1 = pair_of(sem, "added1")
        x_stored = pair_of(sem, "x_stored")
        last_in = pair_of(sem, "last_in")
        out_done = sem("out_done")
        out_stored = pair_of(sem, "out_stored")
        pool_set = sem("pool_set")
        vec_set = sem("vec_set")
        act_set = sem("act_set")
        pe_set = sem("pe_set")
        sp_steps = sem("sp_steps")
        pool_steps = sem("pool_steps")
        act_steps = sem("act_steps")
        pe_steps = sem("pe_steps")

        def hold(eng, steps, semaphore, value):
            eng.wait_ge(semaphore, value)
            eng.sem_inc(steps, 1)

        def ready(b):
            return b + 3

        def free1(b):
            return b + 2

        def free2(b):
            return b + 1

        def run(eng, block_body):
            with eng.Fori(0, LOOPS) as i:
                for s in range(2):
                    block_body(i, s)
            block_body(LOOPS, 0)

        blk = ctx.enter_context(nc.Block())

        @blk.sync
        def _(sp):
            def bc(a, n):
                return a.rearrange("(o n) -> o n", o=1).to_broadcast([P, n])

            sp.dma_start(w1t_sb[:, :], w1t).then_inc(consts_in, 16)
            sp.dma_start(b1_sb[:, :], b1.rearrange("(n o) -> n o", o=1)).then_inc(consts_in, 16)
            sp.dma_start(w2b_sb[:, :], w2b).then_inc(consts_in, 16)
            sp.dma_start(embt_sb[:, :], embt).then_inc(consts_in, 16)
            sp.dma_start(adaptt_sb[:, :], adaptt).then_inc(consts_in, 16)
            sp.dma_start(gamma_b[:, :], bc(gamma, H)).then_inc(consts_in, 16)
            sp.dma_start(beta_b[:, :], bc(beta, H)).then_inc(consts_in, 16)
            sp.dma_start(rb2_b[:, :], bc(rb2, H)).then_inc(consts_in, 16)
            sp.dma_start(rw2_sb[:, :, :], rw2.rearrange("(k p) h -> p k h", p=P)).then_inc(consts_in, 16)
            sp.dma_start(dist_sb[:, :], dist).then_inc(consts_in, 16)

            def in_turns(loads, stores):
                loads(0, 0, True)
                loads(0, 1, True)
                stores(0, 0)
                with sp.Fori(1, LOOPS) as i:
                    loads(i, 0, False)
                    stores(i - 1, 1)
                    loads(i, 1, False)
                    stores(i, 0)
                loads(LOOPS, 0, False)
                stores(LOOPS - 1, 1)
                stores(LOOPS, 0)

            def stage1_loads(i, s, first):
                b = i * 2 + s
                if not first:
                    hold(sp, sp_steps, S["once_done"], free2(b))
                    hold(sp, sp_steps, S["same_done"], free2(b))
                    hold(sp, sp_steps, S["mean_done"], free2(b))
                    hold(sp, sp_steps, kept_stored[s], i * 32)
                sp.dma_start(idx[s][:, :], edge_idx[bass.ds(b, 1)].rearrange("o p t -> (o p) t")).then_inc(idx_in[s], 16)
                sp.dma_start(rows[s][:, :], edge_rows[bass.ds(b, 1)].to_broadcast([P, 2 * BE])).then_inc(rows_in[s], 16)
                if not first:
                    hold(sp, sp_steps, S["h1_done"], free2(b))
                sp.dma_start(feat[s][:, :], edge_feat[bass.ds(b, 1)].rearrange("o f e -> (o f) e")).then_inc(feat_in[s], 16)
                if not first:
                    hold(sp, sp_steps, S["kept_done"], free2(b))
                sp.dma_start(nodes[s][:, 2 * TILES:G1, :].rearrange("p r w -> p (r w)"),
                             table_chunks[bass.ds(b, 1)].rearrange("o p w -> (o p) w")).then_inc(chunk_in[s], 16)

            def stage1_stores(i, s):
                b = i * 2 + s
                hold(sp, sp_steps, S["kept_done"], ready(b))
                hold(sp, sp_steps, S["once_done"], ready(b))
                sp.dma_start(kept[bass.ds(b, 1)].rearrange("o p w -> (o p) w"),
                             kept_out[s][:, :, :].rearrange("p r w -> p (r w)")).then_inc(kept_stored[s], 16)
                sp.dma_start(dst_once[bass.ds(b, 1)].rearrange("o p w -> (o p) w"),
                             once[s][:, 0:TILES]).then_inc(kept_stored[s], 16)

            in_turns(stage1_loads, stage1_stores)

            sp.wait_ge(kept_stored[0], 32 * (LOOPS + 1))
            sp.wait_ge(kept_stored[1], 32 * LOOPS)
            sp.wait_ge(added0[0], ADDS * (LOOPS + 1))
            sp.wait_ge(added0[1], ADDS * LOOPS)

            def stage2_loads(i, s, first):
                b = i * 2 + s
                if not first:
                    hold(sp, sp_steps, S["same1_done"], free2(b))
                    hold(sp, sp_steps, S["msg1_done"], free2(b))
                    hold(sp, sp_steps, S["tot_done"], free2(b))
                    hold(sp, sp_steps, added1[s], i * ADDS)
                    hold(sp, sp_steps, x_stored[s], i * 16)
                sp.dma_start(idx[s][:, :], edge_idx[bass.ds(b, 1)].rearrange("o p t -> (o p) t")).then_inc(idx2_in[s], 16)
                sp.dma_start(didx[s][:, :], dst_once[bass.ds(b, 1)].rearrange("o p t -> (o p) t")).then_inc(idx2_in[s], 16)
                sp.dma_start(rows[s][:, 0:BE], edge_rows[bass.ds(b, 1), 0:BE].to_broadcast([P, BE])).then_inc(rows2_in[s], 16)
                sp.dma_start(edge_sc[s][:, 0:TILES], norm[bass.ds(b, 1)].rearrange("o p t -> (o p) t")).then_inc(rows2_in[s], 16)
                sp.dma_start(edge_sc[s][:, TILES:2 * TILES].bitcast(I32),
                             rel[bass.ds(b, 1)].rearrange("o p t -> (o p) t")).then_inc(rows2_in[s], 16)
                if not first:
                    hold(sp, sp_steps, S["x2_done"], free2(b))
                sp.dma_start(agg_in[s][:, TILES:G2, :].rearrange("p r w -> p (r w)"),
                             agg0_chunks[bass.ds(b, 1)].rearrange("o p w -> (o p) w")).then_inc(agg_chunk_in[s], 16)
                sp.dma_start(kept_in[s][:, :, :].rearrange("p r w -> p (r w)"),
                             kept[bass.ds(b, 1)].rearrange("o p w -> (o p) w")).then_inc(kept_got[s], 16)

            def stage2_stores(i, s):
                b = i * 2 + s
                hold(sp, sp_steps, S["x2_done"], ready(b))
                sp.dma_start(x_mid[bass.ds(b, 1)].rearrange("o p w -> (o p) w"),
                             x2[s][:, TILES:G2, :].rearrange("p r w -> p (r w)")).then_inc(x_stored[s], 16)

            in_turns(stage2_loads, stage2_stores)

            sp.wait_ge(x_stored[0], 16 * (LOOPS + 1))
            sp.wait_ge(x_stored[1], 16 * LOOPS)
            sp.wait_ge(added1[0], ADDS * (LOOPS + 1))
            sp.wait_ge(added1[1], ADDS * LOOPS)

            def stage3_loads(i, s, first):
                b = i * 2 + s
                if not first:
                    hold(sp, sp_steps, out_done, free2(b))
                    hold(sp, sp_steps, out_stored[s], i * 16)
                sp.dma_start(agg_last[s][:, :], agg1_chunks[bass.ds(b, 1)].rearrange("o p w -> (o p) w")).then_inc(last_in[s], 16)
                sp.dma_start(x_last[s][:, :], x_mid[bass.ds(b, 1)].rearrange("o p w -> (o p) w")).then_inc(last_in[s], 16)

            in_turns(stage3_loads, lambda i, s: None)
            sp.wait_ge(out_stored[0], 16 * (LOOPS + 1))
            sp.wait_ge(out_stored[1], 16 * LOOPS)

        @blk.gpsimd
        def _(pool):
            nc.gpsimd.memset(zeros[:, :], 0.0).then_inc(pool_set, 1)
            nc.gpsimd.memset(ident[:, :], 0.0).then_inc(pool_set, 1)
            nc.gpsimd.memset(earlier[:, :], 1.0).then_inc(pool_set, 1)
            nc.gpsimd.memset(rw1_sb[:, :], OFF).then_inc(pool_set, 1)
            nc.gpsimd.memset(gate_in[:, :], 1.0).then_inc(pool_set, 1)
            nc.gpsimd.memset(half_pi[:, :], float(np.pi / 2)).then_inc(pool_set, 1)
            nc.gpsimd.memset(eps[:, :], EPS).then_inc(pool_set, 1)
            nc.gpsimd.iota(iota_type[:, :], pattern=[[1, NTYPE]], base=0, channel_multiplier=0,
                           allow_small_or_imprecise_dtypes=True).then_inc(pool_set, 1)
            nc.gpsimd.iota(iota_rel[:, :], pattern=[[1, NREL]], base=0, channel_multiplier=0,
                           allow_small_or_imprecise_dtypes=True).then_inc(pool_set, 1)
            nc.gpsimd.iota(dump_id[:, :, :], pattern=[[0, TILES], [P, 2]], base=DUMP, channel_multiplier=1,
                           allow_small_or_imprecise_dtypes=True).then_inc(pool_set, 1)
            pool.wait_ge(pool_set, 10)
            nc.gpsimd.affine_select(out=ident[:, :], in_=ident[:, :], compare_op=ALU.not_equal, fill=1.0, base=0,
                                    pattern=[[-1, P]], channel_multiplier=1).then_inc(pool_set, 1)
            nc.gpsimd.affine_select(out=earlier[:, P:2 * P], in_=earlier[:, P:2 * P], compare_op=ALU.is_gt, fill=0.0,
                                    base=0, pattern=[[-1, P]], channel_multiplier=1).then_inc(pool_set, 1)

            def in_turns(gather, add, last_added):
                gather(0, 0, True)
                gather(0, 1, True)
                add(0, 0)
                with pool.Fori(1, LOOPS) as i:
                    gather(i, 0, False)
                    add(i - 1, 1)
                    gather(i, 1, False)
                    add(i, 0)
                gather(LOOPS, 0, False)
                add(LOOPS - 1, 1)
                pool.wait_ge(last_added[1], ADDS * LOOPS)
                add(LOOPS, 0)
                pool.wait_ge(last_added[0], ADDS * (LOOPS + 1))

            def gather_ends(i, s, first):
                b = i * 2 + s
                hold(pool, pool_steps, idx_in[s], (i + 1) * 16)
                if first and s == 1:
                    pool.wait_ge(agg0_set, 16 * NBLOCK)
                if not first:
                    hold(pool, pool_steps, S["kept_done"], free2(b))
                    hold(pool, pool_steps, S["msg_done"], free2(b))
                for t in range(2 * TILES):
                    if t == TILES and not first:
                        hold(pool, adds0_done, added0[s], i * ADDS)
                    pool.indirect_dma_start(nodes[s][:, t, :], None, table,
                                            bass.IndirectOffsetOnAxis(ap=idx[s][:, t:t + 1], axis=0)).then_inc(ends_in[s], 16)

            def add0(i, s):
                b = i * 2 + s
                hold(pool, pool_steps, S["sums_copied"], ready(b))
                hold(pool, pool_steps, S["once_done"], ready(b))
                for q in range(TILES // 2):
                    if q:
                        hold(pool, pool_steps, added0[s], i * ADDS + 32 * q)
                    for t in (2 * q, 2 * q + 1):
                        pool.indirect_dma_start(agg0, bass.IndirectOffsetOnAxis(ap=once[s][:, TILES + t:TILES + t + 1], axis=0),
                                                sums[s][:, t, :], None, compute_op=ALU.add).then_inc(added0[s], 16)

            pool.sem_inc(adds0_done, 2)
            pool.sem_inc(adds1_done, 2)
            in_turns(gather_ends, add0, added0)

            def gather_agg0(i, s, first):
                b = i * 2 + s
                hold(pool, pool_steps, idx2_in[s], (i + 1) * 32)
                if first and s == 1:
                    pool.wait_ge(agg1_set, 16 * NBLOCK)
                if not first:
                    hold(pool, pool_steps, S["ydiv_done"], free2(b))
                for t in range(TILES):
                    if t == TILES // 2 and not first:
                        hold(pool, adds1_done, added1[s], i * ADDS)
                    pool.indirect_dma_start(agg_in[s][:, t, :], None, agg0,
                                            bass.IndirectOffsetOnAxis(ap=idx[s][:, TILES + t:TILES + t + 1], axis=0)).then_inc(agg_ends_in[s], 16)

            def add1(i, s):
                b = i * 2 + s
                hold(pool, pool_steps, S["sums1_copied"], ready(b))
                for q in range(TILES // 2):
                    if q:
                        hold(pool, pool_steps, added1[s], i * ADDS + 32 * q)
                    for t in (2 * q, 2 * q + 1):
                        pool.indirect_dma_start(agg1, bass.IndirectOffsetOnAxis(ap=didx[s][:, t:t + 1], axis=0),
                                                sums1[s][:, t, :], None, compute_op=ALU.add).then_inc(added1[s], 16)

            in_turns(gather_agg0, add1, added1)

        @blk.tensor
        def _(pe):
            for n in ("onehot_t_done", "q_done", "h1_done", "gate_done", "sums_done",
                      "h2t_done", "k1_done", "m1_done", "sums1_done"):
                pe.sem_inc(S[n], 2)
            pe.wait_ge(consts_in, 160)
            nc.tensor.matmul(ps_t[0:GEMB, 0:NTYPE], adaptt_sb[:, :], embt_sb[:, :], start=True, stop=True).then_inc(pe_set, 1)
            pe.wait_ge(vec_set, 1)
            nc.tensor.matmul(ps_q[0:NTYPE, 0:NTYPE], embt_sb[:, :], ada[:, :], start=True, stop=True).then_inc(pe_set, 1)
            pe.wait_ge(pool_set, 12)
            pe.wait_ge(vec_set, 2)

            def stage1(i, s):
                b = i * 2 + s
                hold(pe, pe_steps, feat_in[s], (i + 1) * 16)
                hold(pe, pe_steps, S["gate_in_done"], free1(b))
                nc.tensor.matmul(ps_h[0:H, :], w1t_sb[:, :], feat[s][:, :], start=True, stop=True).then_inc(S["h1_done"], 1)
                hold(pe, pe_steps, S["onehot_done"], ready(b))
                hold(pe, pe_steps, S["onehot_copied"], free1(b))
                for t in range(TILES):
                    last = nc.tensor.transpose(ps_t[0:NTYPE, t * P:(t + 1) * P], onehot[:, t, :], ident[:, :])
                last.then_inc(S["onehot_t_done"], 1)
                hold(pe, pe_steps, S["gate_in_done"], ready(b))
                hold(pe, pe_steps, S["msg_done"], free1(b))
                for t in range(TILES):
                    last = nc.tensor.matmul(ps_m[:, t * H:(t + 1) * H], gate_in[0:H + 1, t * P:(t + 1) * P], w2b_sb[:, :],
                                            start=True, stop=True)
                last.then_inc(S["gate_done"], 1)
                hold(pe, pe_steps, S["onehot_copied"], ready(b))
                hold(pe, pe_steps, S["logit_done"], free1(b))
                for t in range(TILES):
                    last = nc.tensor.matmul(ps_q[:, t * NTYPE:(t + 1) * NTYPE], onehot_t[:, t, :], q_sb[:, :], start=True, stop=True)
                last.then_inc(S["q_done"], 1)
                hold(pe, pe_steps, S["msg_done"], ready(b))
                hold(pe, pe_steps, S["same_done"], ready(b))
                hold(pe, pe_steps, S["sums_copied"], free1(b))
                for q in range(TILES // 2):
                    a = 2 * q
                    nc.tensor.matmul(ps_s[:, a * AW:(a + 1) * AW], same_a[:, q, :], msg[:, a, :], start=True, stop=False)
                    nc.tensor.matmul(ps_s[:, a * AW:(a + 1) * AW], same_b[:, q, 0:P], msg[:, a + 1, :], start=False, stop=True)
                    last = nc.tensor.matmul(ps_s[:, (a + 1) * AW:(a + 2) * AW], same_b[:, q, P:2 * P], msg[:, a + 1, :],
                                            start=True, stop=True)
                last.then_inc(S["sums_done"], 1)

            run(pe, stage1)
            pe.wait_ge(rw1_in, 16)
            pe.wait_ge(rb1_in, 16 * NREL)

            def stage2(i, s):
                b = i * 2 + s
                hold(pe, pe_steps, S["h2_done"], ready(b))
                hold(pe, pe_steps, S["rel_done"], ready(b))
                hold(pe, pe_steps, S["h2t_copied"], free1(b))
                for t in range(TILES):
                    last = nc.tensor.transpose(ps_t[0:H + NREL, t * P:(t + 1) * P], h2[:, t, :], ident[:, :])
                last.then_inc(S["h2t_done"], 1)
                hold(pe, pe_steps, S["h2t_copied"], ready(b))
                hold(pe, pe_steps, S["hid1_done"], free1(b))
                for k in range(KC):
                    last = nc.tensor.matmul(ps_k[k][:, :], rw1_sb[:, k * P:(k + 1) * P], h2_t[:, :], start=True, stop=True)
                last.then_inc(S["k1_done"], 1)
                hold(pe, pe_steps, S["hid1_done"], ready(b))
                hold(pe, pe_steps, S["msg1_done"], free1(b))
                for t in range(TILES):
                    for k in range(KC):
                        last = nc.tensor.matmul(ps_m[:, t * H:(t + 1) * H], hid1[:, k, t * P:(t + 1) * P], rw2_sb[:, k, :],
                                                start=(k == 0), stop=(k == KC - 1))
                last.then_inc(S["m1_done"], 1)
                hold(pe, pe_steps, S["msg1_done"], ready(b))
                hold(pe, pe_steps, S["same1_done"], ready(b))
                hold(pe, pe_steps, S["sums1_copied"], free1(b))
                for q in range(TILES // 2):
                    a = 2 * q
                    nc.tensor.matmul(ps_s[:, a * H:(a + 1) * H], same_a[:, q, :], msg1[:, a, :], start=True, stop=False)
                    nc.tensor.matmul(ps_s[:, a * H:(a + 1) * H], same_b[:, q, 0:P], msg1[:, a + 1, :], start=False, stop=True)
                    last = nc.tensor.matmul(ps_s[:, (a + 1) * H:(a + 2) * H], same_b[:, q, P:2 * P], msg1[:, a + 1, :],
                                            start=True, stop=True)
                last.then_inc(S["sums1_done"], 1)

            run(pe, stage2)

        @blk.scalar
        def _(act):
            for n in ("onehot_copied", "gate_in_done", "sq_done", "std_done", "hid_done", "sums_copied", "ysq_done",
                      "ystd_done", "esq_done", "estd_done", "h2_done", "h2t_copied", "hid1_done", "sums1_copied"):
                act.sem_inc(S[n], 2)
            act.wait_ge(pool_set, 10)
            with act.Fori(0, NBLOCK) as c:
                act.dma_start(agg0_chunks[bass.ds(c, 1)].rearrange("o p w -> (o p) w"), zeros[:, :]).then_inc(agg0_set, 16)
            act.dma_start(rw1_sb[0:H, :], rw1).then_inc(rw1_in, 16)
            for r in range(NREL):
                act.dma_start(rw1_sb[H + r:H + r + 1, r * H:(r + 1) * H], rb1.rearrange("(o n) -> o n", o=1)).then_inc(rb1_in, 16)
            act.wait_ge(vec_set, 3)
            with act.Fori(0, NBLOCK) as c:
                act.dma_start(agg1_chunks[bass.ds(c, 1)].rearrange("o p w -> (o p) w"),
                              bias_rows[:, :, :].rearrange("p r w -> p (r w)")).then_inc(agg1_set, 16)
            act.wait_ge(vec_set, 4)
            nc.scalar.activation(cw_b[:, :], cw_a[:, :], ACT.Sin, bias=half_pi[:, :], scale=-float(np.pi) / CUTOFF).then_inc(act_set, 1)

            def stage1(i, s):
                b = i * 2 + s
                hold(act, act_steps, S["h1_done"], ready(b))
                hold(act, act_steps, S["gate_done"], free1(b))
                nc.scalar.activation(gate_in[0:H, :], ps_h[0:H, :], ACT.Silu, bias=b1_sb[:, :], scale=1.0).then_inc(S["gate_in_done"], 1)
                hold(act, act_steps, S["onehot_t_done"], ready(b))
                hold(act, act_steps, S["q_done"], free1(b))
                nc.scalar.copy(onehot_t[:, :, :].rearrange("p t e -> p (t e)"), ps_t[0:NTYPE, :]).then_inc(S["onehot_copied"], 1)
                hold(act, act_steps, S["cen_done"], ready(b))
                hold(act, act_steps, S["var_done"], free1(b))
                nc.scalar.activation(sq[:, :, :], cen[:, :, :], ACT.Square).then_inc(S["sq_done"], 1)
                hold(act, act_steps, S["var_done"], ready(b))
                hold(act, act_steps, S["rstd_done"], free1(b))
                nc.scalar.activation(std[:, :], var[:, :], ACT.Sqrt, bias=eps[:, :], scale=1.0 / H).then_inc(S["std_done"], 1)
                hold(act, act_steps, S["nrm_done"], ready(b))
                hold(act, act_steps, S["kept_done"], free1(b))
                hold(act, act_steps, S["hdst_done"], free1(b))
                nc.scalar.activation(hid[:, :, :], nrm[:, :, :], ACT.Relu).then_inc(S["hid_done"], 1)
                hold(act, act_steps, S["sums_done"], ready(b))
                hold(act, act_steps, adds0_done, free2(b))
                nc.scalar.copy(sums[s][:, :, :].rearrange("p t w -> p (t w)"), ps_s[:, 0:TILES * AW]).then_inc(S["sums_copied"], 1)

            run(act, stage1)

            def stage2(i, s):
                b = i * 2 + s
                hold(act, act_steps, S["ycen_done"], ready(b))
                hold(act, act_steps, S["yvar_done"], free1(b))
                nc.scalar.activation(ysq[:, :, :], ycen2[:, :, :], ACT.Square).then_inc(S["ysq_done"], 1)
                hold(act, act_steps, S["yvar_done"], ready(b))
                hold(act, act_steps, S["yrstd_done"], free1(b))
                nc.scalar.activation(ystd[:, :], yvar[:, :], ACT.Sqrt, bias=eps[:, :], scale=1.0 / H).then_inc(S["ystd_done"], 1)
                hold(act, act_steps, S["ecen_done"], ready(b))
                hold(act, act_steps, S["evar_done"], free1(b))
                nc.scalar.activation(sq[:, 0:TILES, :], cen[:, 0:TILES, :], ACT.Square).then_inc(S["esq_done"], 1)
                hold(act, act_steps, S["evar_done"], ready(b))
                hold(act, act_steps, S["erstd_done"], free1(b))
                nc.scalar.activation(std[:, 0:TILES], var[:, 0:TILES], ACT.Sqrt, bias=eps[:, :], scale=1.0 / H).then_inc(S["estd_done"], 1)
                hold(act, act_steps, S["enrm_done"], ready(b))
                hold(act, act_steps, S["h2t_done"], free1(b))
                nc.scalar.activation(h2[:, :, 0:H], h2n[:, :, :], ACT.Relu).then_inc(S["h2_done"], 1)
                hold(act, act_steps, S["h2t_done"], ready(b))
                hold(act, act_steps, S["k1_done"], free1(b))
                nc.scalar.copy(h2_t[:, :], ps_t[0:H + NREL, :]).then_inc(S["h2t_copied"], 1)
                hold(act, act_steps, S["k1_done"], ready(b))
                hold(act, act_steps, S["m1_done"], free1(b))
                for k in range(KC):
                    last = nc.scalar.activation(hid1[:, k, :], ps_k[k][:, :], ACT.Relu)
                last.then_inc(S["hid1_done"], 1)
                hold(act, act_steps, S["sums1_done"], ready(b))
                hold(act, act_steps, adds1_done, free2(b))
                nc.scalar.copy(sums1[s][:, :, :].rearrange("p t w -> p (t w)"), ps_s[:, 0:TILES * H]).then_inc(S["sums1_copied"], 1)

            run(act, stage2)

            def stage3(i, s):
                b = i * 2 + s
                hold(act, act_steps, out_done, ready(b))
                act.dma_start(out_chunks[bass.ds(b, 1)].rearrange("o p w -> (o p) w"), out_sb[s][:, :]).then_inc(out_stored[s], 16)

            run(act, stage3)

        @blk.vector
        def _(dve):
            for n in ("mean_done nmean_done cen_done var_done rstd_done nrm_done hsum_done hmean_done kept_done "
                      "ahead_done turn_done turned_done once_done same_done onehot_done logit_done coef_done hdst_done "
                      "raw_done mmean_done msg_done tot_done rtot_done ydiv_done ycen_done yvar_done yrstd_done "
                      "ynrm_done ygam_done x2_done esum_done emean_done ecen_done evar_done erstd_done enrm_done "
                      "rel_done msg1_done same1_done").split():
                dve.sem_inc(S[n], 2)
            dve.sem_inc(out_done, 2)

            V = nc.vector

            def cols(a, n):
                return a.unsqueeze(2).to_broadcast([P, a.shape[1], n])

            def each(a, n):
                return a.unsqueeze(1).to_broadcast([P, n, a.shape[1]])

            dve.wait_ge(pe_set, 1)
            V.tensor_copy(ada[:, :], ps_t[0:GEMB, 0:NTYPE]).then_inc(vec_set, 1)
            dve.wait_ge(pe_set, 2)
            V.tensor_copy(q_sb[:, :], ps_q[0:NTYPE, 0:NTYPE]).then_inc(vec_set, 1)
            dve.wait_ge(consts_in, 160)
            V.tensor_copy(bias_rows[:, :, :], each(rb2_b[:, :], NR)).then_inc(vec_set, 1)
            V.tensor_scalar(cw_all[:, :], dist_sb[:, :], -1.0, CUTOFF, ALU.mult, ALU.min).then_inc(act_set, 1)
            V.tensor_scalar(cw_b[:, :], dist_sb[:, :], CUTOFF, None, ALU.min).then_inc(act_set, 1)
            dve.wait_ge(act_set, 2)
            V.tensor_tensor(cw_a[:, :], cw_all[:, :], cw_b[:, :], ALU.max).then_inc(vec_set, 1)
            dve.wait_ge(act_set, 3)
            V.tensor_scalar(cw_a[:, :], cw_b[:, :], 1.0, 0.5, ALU.add, ALU.mult).then_inc(act_set, 1)
            dve.wait_ge(act_set, 4)
            V.scalar_tensor_tensor(out=cw_all[:, :], in0=dist_sb[:, :], scalar=CUTOFF, in1=cw_a[:, :],
                                   op0=ALU.is_lt, op1=ALU.mult).then_inc(act_set, 1)
            dve.wait_ge(act_set, 5)
            dve.wait_ge(pool_set, 12)

            def same_node(slot, first_col, done, b):
                for q in range(TILES // 2):
                    a = 2 * q
                    at = first_col * P
                    V.tensor_scalar(same_a[:, q, :], rows[slot][:, at + a * P:at + (a + 1) * P],
                                    idx[slot][:, first_col + a:first_col + a + 1], None, ALU.is_equal)
                    last = V.tensor_scalar(same_b[:, q, :], rows[slot][:, at + a * P:at + (a + 2) * P],
                                           idx[slot][:, first_col + a + 1:first_col + a + 2], None, ALU.is_equal)
                last.then_inc(S[done], 1)

            def stage1(i, s):
                b = i * 2 + s
                dve.wait_ge(idx_in[s], (i + 1) * 16)
                dve.wait_ge(rows_in[s], (i + 1) * 16)
                for t in range(2 * TILES):
                    a = t - t % 2
                    n = P * (1 + t % 2)
                    last = V.scalar_tensor_tensor(out=junk[:, t, 0:n], in0=rows[s][:, a * P:a * P + n], scalar=idx[s][:, t:t + 1],
                                                  in1=earlier[:, 2 * P - n:2 * P], op0=ALU.is_equal, op1=ALU.mult,
                                                  accum_out=ahead[:, t:t + 1])
                last.then_inc(S["ahead_done"], 1)
                V.tensor_tensor(turn[:, :], dump_id[:, :, :].rearrange("p a b -> p (a b)"), idx[s][:, :], ALU.subtract).then_inc(S["turn_done"], 1)
                dve.wait_ge(S["sums_done"], free1(b))
                same_node(s, TILES, "same_done", b)
                dve.wait_ge(S["ahead_done"], ready(b))
                dve.wait_ge(S["turn_done"], ready(b))
                V.scalar_tensor_tensor(out=turned[:, :], in0=ahead[:, :], scalar=0.0, in1=turn[:, :], op0=ALU.is_gt,
                                       op1=ALU.mult).then_inc(S["turned_done"], 1)
                dve.wait_ge(S["turned_done"], ready(b))
                dve.wait_ge(adds0_done, free2(b))
                V.tensor_tensor(once[s][:, :], idx[s][:, :], turned[:, :], ALU.add).then_inc(S["once_done"], 1)
                dve.wait_ge(ends_in[s], (i + 1) * (2 * TILES * 16))
                dve.wait_ge(chunk_in[s], (i + 1) * 16)
                x = nodes[s][:, :, 0:H]
                V.tensor_reduce(stat[:, :], x, AX_X, ALU.add).then_inc(S["mean_done"], 1)
                dve.wait_ge(S["onehot_t_done"], free1(b))
                V.tensor_tensor(onehot[:, :, :], each(iota_type[:, :], TILES),
                                nodes[s][:, TILES:2 * TILES, H + 1:H + 2].bitcast(I32).to_broadcast([P, TILES, NTYPE]),
                                ALU.is_equal).then_inc(S["onehot_done"], 1)
                dve.wait_ge(S["mean_done"], ready(b))
                V.tensor_scalar(nmean[:, :], stat[:, :], -1.0 / H, None, ALU.mult).then_inc(S["nmean_done"], 1)
                dve.wait_ge(S["nmean_done"], ready(b))
                V.tensor_tensor(cen[:, :, :], x, cols(nmean[:, :], H), ALU.add).then_inc(S["cen_done"], 1)
                xb = nodes[s][:, TILES:G1, 0:H]
                V.tensor_tensor(kept_out[s][:, :, H:HW], xb, each(beta_b[:, :], G2), ALU.add)
                node_w = nodes[s][:, 0:TILES, H:H + 1].rearrange("p t o -> p (t o)")
                V.tensor_tensor(coef[:, :], node_w, cw_all[:, bass.ds(b * TILES, TILES)], ALU.mult).then_inc(S["coef_done"], 1)
                dve.wait_ge(S["sq_done"], ready(b))
                V.tensor_reduce(var[:, :], sq[:, :, :], AX_X, ALU.add).then_inc(S["var_done"], 1)
                dve.wait_ge(S["q_done"], ready(b))
                for t in range(TILES):
                    last = V.scalar_tensor_tensor(out=junk_q[:, t, :], in0=iota_type[:, :],
                                                  scalar=nodes[s][:, t, H + 1:H + 2].bitcast(I32),
                                                  in1=ps_q[:, t * NTYPE:(t + 1) * NTYPE], op0=ALU.is_equal, op1=ALU.mult,
                                                  accum_out=logit[:, t:t + 1])
                last.then_inc(S["logit_done"], 1)
                dve.wait_ge(S["std_done"], ready(b))
                V.reciprocal(rstd[:, :], std[:, :]).then_inc(S["rstd_done"], 1)
                dve.wait_ge(S["rstd_done"], ready(b))
                V.tensor_tensor(nrm[:, :, :], cen[:, :, :], cols(rstd[:, :], H), ALU.mult).then_inc(S["nrm_done"], 1)
                dve.wait_ge(S["coef_done"], ready(b))
                dve.wait_ge(S["hid_done"], ready(b))
                V.tensor_tensor(hdst[:, :, :], hid[:, 0:TILES, :], cols(coef[:, :], H), ALU.mult).then_inc(S["hdst_done"], 1)
                dve.wait_ge(S["logit_done"], ready(b))
                dve.wait_ge(S["hdst_done"], ready(b))
                dve.wait_ge(S["gate_done"], ready(b))
                for t in range(TILES):
                    last = V.scalar_tensor_tensor(out=msg_raw[:, t, :], in0=ps_m[:, t * H:(t + 1) * H], scalar=logit[:, t:t + 1],
                                                  in1=hdst[:, t, :], op0=ALU.add, op1=ALU.mult, accum_out=msum[:, t:t + 1])
                last.then_inc(S["raw_done"], 1)
                V.tensor_reduce(hsum[:, :], hid[:, TILES:G1, :], AX_X, ALU.add).then_inc(S["hsum_done"], 1)
                dve.wait_ge(S["raw_done"], ready(b))
                V.tensor_scalar(mmean[:, :], msum[:, :], -1.0 / H, None, ALU.mult).then_inc(S["mmean_done"], 1)
                dve.wait_ge(S["hsum_done"], ready(b))
                V.tensor_scalar(hmean[:, :], hsum[:, :], -1.0 / H, None, ALU.mult).then_inc(S["hmean_done"], 1)
                dve.wait_ge(S["mmean_done"], ready(b))
                V.tensor_copy(msg[:, :, H:AW], nodes[s][:, 0:TILES, H:H + 1])
                V.tensor_tensor(msg[:, :, 0:H], msg_raw[:, :, :], cols(mmean[:, :], H), ALU.add).then_inc(S["msg_done"], 1)
                dve.wait_ge(S["hmean_done"], ready(b))
                V.tensor_tensor(kept_out[s][:, :, 0:H], hid[:, TILES:G1, :], cols(hmean[:, :], H), ALU.add).then_inc(S["kept_done"], 1)

            run(dve, stage1)

            def stage2(i, s):
                b = i * 2 + s
                dve.wait_ge(agg_chunk_in[s], (i + 1) * 16)
                dve.wait_ge(agg_ends_in[s], (i + 1) * (TILES * 16))
                V.tensor_scalar(tot[:, :], agg_in[s][:, :, H:AW].rearrange("p r o -> p (r o)"), 1e-8, None, ALU.max).then_inc(S["tot_done"], 1)
                dve.wait_ge(S["tot_done"], ready(b))
                V.reciprocal(rtot[:, :], tot[:, :]).then_inc(S["rtot_done"], 1)
                dve.wait_ge(S["rtot_done"], ready(b))
                V.tensor_tensor(ycen[:, :, :], agg_in[s][:, :, 0:H], cols(rtot[:, :], H), ALU.mult).then_inc(S["ydiv_done"], 1)
                dve.wait_ge(S["ydiv_done"], ready(b))
                dve.wait_ge(kept_got[s], (i + 1) * 16)
                V.tensor_tensor(ycen2[:, :, :], ycen[:, :, :], kept_in[s][:, :, 0:H], ALU.add).then_inc(S["ycen_done"], 1)
                dve.wait_ge(idx2_in[s], (i + 1) * 32)
                dve.wait_ge(rows2_in[s], (i + 1) * 48)
                dve.wait_ge(S["sums1_done"], free1(b))
                same_node(s, 0, "same1_done", b)
                dve.wait_ge(S["h2t_done"], free1(b))
                V.tensor_tensor(h2[:, :, H:H + NREL], each(iota_rel[:, :], TILES),
                                edge_sc[s][:, TILES:2 * TILES].bitcast(I32).unsqueeze(2).to_broadcast([P, TILES, NREL]),
                                ALU.is_equal).then_inc(S["rel_done"], 1)
                dve.wait_ge(S["ysq_done"], ready(b))
                V.tensor_reduce(yvar[:, :], ysq[:, :, :], AX_X, ALU.add).then_inc(S["yvar_done"], 1)
                dve.wait_ge(S["ystd_done"], ready(b))
                V.reciprocal(yrstd[:, :], ystd[:, :]).then_inc(S["yrstd_done"], 1)
                dve.wait_ge(S["yrstd_done"], ready(b))
                V.tensor_tensor(ynrm[:, :, :], ycen2[:, :, :], cols(yrstd[:, :], H), ALU.mult).then_inc(S["ynrm_done"], 1)
                dve.wait_ge(S["ynrm_done"], ready(b))
                V.tensor_tensor(ygam[:, :, :], ynrm[:, :, :], each(gamma_b[:, :], G2), ALU.mult).then_inc(S["ygam_done"], 1)
                dve.wait_ge(S["ygam_done"], ready(b))
                V.tensor_tensor(x2[s][:, :, :], ygam[:, :, :], kept_in[s][:, :, H:HW], ALU.add).then_inc(S["x2_done"], 1)
                dve.wait_ge(S["x2_done"], ready(b))
                V.tensor_reduce(stat[:, 0:TILES], x2[s][:, 0:TILES, :], AX_X, ALU.add).then_inc(S["esum_done"], 1)
                dve.wait_ge(S["esum_done"], ready(b))
                V.tensor_scalar(nmean[:, 0:TILES], stat[:, 0:TILES], -1.0 / H, None, ALU.mult).then_inc(S["emean_done"], 1)
                dve.wait_ge(S["emean_done"], ready(b))
                V.tensor_tensor(cen[:, 0:TILES, :], x2[s][:, 0:TILES, :], cols(nmean[:, 0:TILES], H), ALU.add).then_inc(S["ecen_done"], 1)
                dve.wait_ge(S["esq_done"], ready(b))
                V.tensor_reduce(var[:, 0:TILES], sq[:, 0:TILES, :], AX_X, ALU.add).then_inc(S["evar_done"], 1)
                dve.wait_ge(S["estd_done"], ready(b))
                V.reciprocal(rstd[:, 0:TILES], std[:, 0:TILES]).then_inc(S["erstd_done"], 1)
                dve.wait_ge(S["erstd_done"], ready(b))
                V.tensor_tensor(h2n[:, :, :], cen[:, 0:TILES, :], cols(rstd[:, 0:TILES], H), ALU.mult).then_inc(S["enrm_done"], 1)
                dve.wait_ge(S["m1_done"], ready(b))
                V.tensor_tensor(msg1[:, :, :], ps_m[:, 0:TILES * H].rearrange("p (t h) -> p t h", t=TILES),
                                cols(edge_sc[s][:, 0:TILES], H), ALU.mult).then_inc(S["msg1_done"], 1)

            run(dve, stage2)

            def stage3(i, s):
                dve.wait_ge(last_in[s], (i + 1) * 32)
                V.scalar_tensor_tensor(out=out_sb[s][:, :], in0=agg_last[s][:, :], scalar=0.0, in1=x_last[s][:, :],
                                       op0=ALU.max, op1=ALU.add).then_inc(out_done, 1)

            run(dve, stage3)


def kernel(**inputs):
    import concourse.bacc as bacc
    from concourse.bass_utils import run_bass_kernel_spmd

    a = {k: np.asarray(v) for k, v in inputs.items()}
    ep = NBLOCK * BE

    def edges(v, fill=0):
        full = np.full((ep,), fill, v.dtype)
        full[:E] = v.reshape(-1)
        return full.reshape(NBLOCK, TILES, P)

    def columns(v):
        return v.transpose(0, 2, 1)

    src, dst = edges(a["src"], NULL), edges(a["dst"], NULL)
    table = np.zeros((NP, TW), np.float32)
    table[:N, :H] = a["x"]
    table[:N, H] = a["node_vec"]
    table[:N, H + 1] = a["node_type_119"].astype(np.int32).view(np.float32)
    feat = np.zeros((ep, RAD), np.float32)
    feat[:E] = a["edge_attr_40"]
    arrays = {
        "table": table,
        "edge_idx": np.concatenate([columns(dst), columns(src)], 2),
        "edge_rows": np.concatenate([dst.reshape(NBLOCK, BE), src.reshape(NBLOCK, BE)], 1),
        "edge_feat": feat.reshape(NBLOCK, BE, RAD).transpose(0, 2, 1),
        "dist": columns(edges(a["edge_weight"])).transpose(1, 0, 2).reshape(P, NBLOCK * TILES),
        "norm": columns(edges(a["edge_weight1"])),
        "rel": columns(edges(a["edge_type_8"])),
        "w1t": a["L0_gnn_W1"].T,
        "b1": a["L0_gnn_b1"],
        "w2b": np.concatenate([a["L0_gnn_W2"].T, a["L0_gnn_b2"][None]], 0),
        "embt": a["L0_gnn_emb"].T,
        "adaptt": a["L0_gnn_adaptW"].T,
        "gamma": a["L0_gnn_gamma"],
        "beta": a["L0_gnn_beta"],
        "rw1": a["L1_gnn_weight1"].transpose(1, 0, 2).reshape(H, CW1),
        "rb1": a["L1_gnn_bias1"],
        "rw2": a["L1_gnn_weight2"].reshape(CW1, H),
        "rb2": a["L1_gnn_bias2"],
    }
    nc = bacc.Bacc("TRN2", target_bir_lowering=False, num_devices=1)
    given, aps = {}, []
    for name, v in arrays.items():
        v = np.ascontiguousarray(v)
        given[f"in_{name}"] = v
        aps.append(nc.dram_tensor(f"in_{name}", v.shape, mybir.dt.from_np(v.dtype), kind="ExternalInput").ap())
    out = nc.dram_tensor("out_0", (NP, H), F32, kind="ExternalOutput").ap()
    build(nc, *aps, out)
    r = run_bass_kernel_spmd(nc, [given], core_ids=[0])
    return r.results[0]["out_0"][:N]
```

```python
from contextlib import ExitStack

import concourse.bass as bass
from concourse import mybir
import numpy as np

F32 = mybir.dt.float32
I32 = mybir.dt.int32
ALU = mybir.AluOpType
ACT = mybir.ActivationFunctionType
CONSTS = 13 * 16
AX_X = mybir.AxisListType.X

P = 128
N = 100000
E = 25000
H = 48
RAD = 40
NREL = 8
NTYPE = 119
GEMB = 32
CUTOFF = 6.0
EPS = 1e-5

TILES = 4
BE = TILES * P
NBLOCK = -(-E // BE)
NR = 16
NP = NBLOCK * P * NR
NULL = N
DUMP = NP - 2 * P
assert NULL < DUMP and NP >= N
TW = H + 2
AW = H + 1
HW = 2 * H
G1 = 2 * TILES + NR
G2 = TILES + NR
CW1 = NREL * H
KC = CW1 // P
OFF = -1.0e30
ADDS = 16 * TILES
HALF = 64
LOOPS = NBLOCK // 2
assert NBLOCK == 2 * LOOPS + 1 and CW1 == KC * P


def build(nc, table, edge_idx, edge_rows, edge_feat, dist, norm, rel, w1t, b1, w2b, embt, adaptt,
          gamma, beta, rw1, rb1, rw2, rb2, out):
    agg0 = nc.dram_tensor("agg0", [NP, AW], F32).ap()
    agg1 = nc.dram_tensor("agg1", [NP, H], F32).ap()
    kept = nc.dram_tensor("kept", [NBLOCK, P, G2 * HW], F32).ap()
    x_mid = nc.dram_tensor("x_mid", [NBLOCK, P, NR * H], F32).ap()
    table_chunks = table.rearrange("(c p r) w -> c p (r w)", p=P, r=NR)
    agg0_chunks = agg0.rearrange("(c p r) w -> c p (r w)", p=P, r=NR)
    agg1_chunks = agg1.rearrange("(c p r) w -> c p (r w)", p=P, r=NR)
    out_chunks = out.rearrange("(c p r) w -> c p (r w)", p=P, r=NR)

    with ExitStack() as ctx:
        def sb(name, shape, dt=F32):
            return ctx.enter_context(nc.sbuf_tensor(name, shape, dt))

        def sem(name):
            return ctx.enter_context(nc.semaphore(name))

        def pair_of(make, name, *args):
            return [make(f"{name}_{s}", *args) for s in range(2)]

        ident = sb("ident", [P, P])
        iota_type = sb("iota_type", [P, NTYPE])
        iota_rel = sb("iota_rel", [P, NREL])
        earlier = sb("earlier", [P, 2 * P])
        dump_id = sb("dump_id", [P, TILES // 2, 2])
        zeros = sb("zeros", [P, NR * AW])
        bias_rows = sb("bias_rows", [P, NR, H])
        half_pi = sb("half_pi", [P, 1])
        eps = sb("eps", [P, 1])
        w1t_sb = sb("w1t_sb", [RAD, H])
        b1_sb = sb("b1_sb", [P, 1])
        w2b_sb = sb("w2b_sb", [P, H])
        embt_sb = sb("embt_sb", [GEMB, NTYPE])
        adaptt_sb = sb("adaptt_sb", [GEMB, GEMB])
        ada = sb("ada", [GEMB, NTYPE])
        q_sb = sb("q_sb", [NTYPE, NTYPE])
        gamma_b = sb("gamma_b", [P, H])
        beta_b = sb("beta_b", [P, H])
        rb2_b = sb("rb2_b", [P, H])
        rw1_sb = sb("rw1_sb", [H + NREL, CW1])
        rw2_sb = sb("rw2_sb", [P, KC, HALF])
        dist_sb = sb("dist_sb", [P, NBLOCK * TILES])
        cw_a = sb("cw_a", [P, NBLOCK * TILES])
        cw_b = sb("cw_b", [P, NBLOCK * TILES])
        cw_all = sb("cw_all", [P, NBLOCK * TILES])

        idx = pair_of(sb, "idx", [P, 2 * TILES], I32)
        rows = pair_of(sb, "rows", [P, BE], I32)
        feat = pair_of(sb, "feat", [RAD, BE])
        nodes = pair_of(sb, "nodes", [P, G1, TW])
        once = pair_of(sb, "once", [P, TILES], I32)
        kept_out = pair_of(sb, "kept_out", [P, G2, HW])
        sums = pair_of(sb, "sums", [P, TILES, AW])
        stats = sb("stats", [P, G1, 6])
        mean2 = sb("mean2", [P, G1])
        mdiff = sb("mdiff", [P, G1])
        vsum = sb("vsum", [P, G1])
        vmix = sb("vmix", [P, G1])
        var = sb("var", [P, G1])
        std = sb("std", [P, G1])
        rstd = sb("rstd", [P, G1])
        shift = sb("shift", [P, G1])
        hid = pair_of(sb, "hid", [P, G1, H])
        hsum = pair_of(sb, "hsum", [P, G2])
        hmean = sb("hmean", [P, G2])
        same_a = pair_of(sb, "same_a", [P, 2, P])
        same_b = pair_of(sb, "same_b", [P, 2, 2 * P])
        junk = sb("junk", [P, TILES, 2 * P])
        junk_q = sb("junk_q", [P, TILES, NTYPE])
        ahead = sb("ahead", [P, TILES])
        turn = sb("turn", [P, TILES])
        turned = sb("turned", [P, TILES])
        onehot = sb("onehot", [P, TILES, NTYPE])
        onehot_t = sb("onehot_t", [NTYPE, TILES, P])
        gate_in = sb("gate_in", [P, BE // 2])
        logit = sb("logit", [P, TILES])
        coef = sb("coef", [P, TILES])
        hdst = sb("hdst", [P, TILES, H])
        msg_raw = sb("msg_raw", [P, TILES, H])
        msum = sb("msum", [P, TILES])
        mmean = sb("mmean", [P, TILES])
        msg = sb("msg", [P, TILES, AW])
        agg_in = pair_of(sb, "agg_in", [P, G2, AW])
        kept_in = pair_of(sb, "kept_in", [P, G2, HW])
        norm_all = sb("norm_all", [P, NBLOCK * TILES])
        rel_all = sb("rel_all", [P, NBLOCK * TILES], I32)
        dkey = pair_of(sb, "dkey", [P, TILES], I32)
        once1 = pair_of(sb, "once1", [P, TILES], I32)
        stat = sb("stat", [P, TILES])
        nmean = sb("nmean", [P, TILES])
        cen = sb("cen", [P, TILES, H])
        sq = sb("sq", [P, TILES, H])
        evar = sb("evar", [P, TILES])
        estd = sb("estd", [P, TILES])
        erstd = sb("erstd", [P, TILES])
        junk1 = sb("junk1", [P, TILES, 2 * P])
        ahead1 = sb("ahead1", [P, TILES])
        turn1 = sb("turn1", [P, TILES])
        turned1 = sb("turned1", [P, TILES])
        x2 = pair_of(sb, "x2", [P, G2, H])
        sums1 = pair_of(sb, "sums1", [P, TILES, H])
        tot = sb("tot", [P, G2])
        rtot = sb("rtot", [P, G2])
        ycen = sb("ycen", [P, G2, H])
        ycen2 = sb("ycen2", [P, G2, H])
        ysq = sb("ysq", [P, G2, H])
        yvar = sb("yvar", [P, G2])
        ystd = sb("ystd", [P, G2])
        yrstd = sb("yrstd", [P, G2])
        ynrm = sb("ynrm", [P, G2, H])
        ygam = sb("ygam", [P, G2, H])
        h2 = sb("h2", [P, TILES, H + NREL])
        h2n = sb("h2n", [P, TILES, H])
        h2_t = sb("h2_t", [H + NREL, BE])
        hid1 = sb("hid1", [P, KC, BE])
        msg1_t = sb("msg1_t", [P, BE // 2])
        msg1 = sb("msg1", [P, TILES, H])
        agg_last = pair_of(sb, "agg_last", [P, NR * H])
        x_last = pair_of(sb, "x_last", [P, NR * H])
        out_sb = pair_of(sb, "out_sb", [P, NR * H])

        def psum(name, shape):
            return ctx.enter_context(nc.psum_tensor(name, shape, F32))

        ps_t = psum("ps_t", [P, 512])
        ps_q = psum("ps_q", [P, 512])
        ps_h = psum("ps_h", [P, 512])
        ps_m = psum("ps_m", [P, 512])
        ps_s = psum("ps_s", [P, 512])
        ps_k = [psum(f"ps_k{k}", [P, 512]) for k in range(KC)]

        consts_in = sem("consts_in")
        rw1_in = sem("rw1_in")
        rb1_in = sem("rb1_in")
        agg0_set = sem("agg0_set")
        agg1_set = sem("agg1_set")
        idx_in = pair_of(sem, "idx_in")
        feat_in = pair_of(sem, "feat_in")
        rows_in = pair_of(sem, "rows_in")
        chunk_in = pair_of(sem, "chunk_in")
        ends_in = pair_of(sem, "ends_in")
        added0 = pair_of(sem, "added0")
        kept_stored = pair_of(sem, "kept_stored")
        names1 = ("stats_done mean2_done mdiff_done vsum_done vmix_done var_done std_done rstd_done shift_done "
                  "hid_dst_done hid_done "
                  "hmean_done kept_done ahead_done turn_done turned_done once_done same_done "
                  "onehot_done onehot_t_done onehot_copied q_done logit_done h1_done gate_in_done gate_done "
                  "coef_done hdst_done raw_done mmean_done msg_done sums_done sums_copied").split()
        names2 = ("tot_done rtot_done ydiv_done ycen_done ysq_done yvar_done ystd_done yrstd_done ynrm_done "
                  "ygam_done x2_done esum_done emean_done ecen_done esq_done evar_done estd_done erstd_done "
                  "enrm_done h2_done rel_done h2t_done h2t_copied k0_done k1_done k2_done relu0_done relu1_done relu2_done "
                  "m1_done m1_copied m1t_done msg1_done same1_done ahead1_done turn1_done turned1_done once1_done "
                  "sums1_done sums1_copied").split()
        S = {n: sem(n) for n in names1 + names2}
        agg_chunk_in = pair_of(sem, "agg_chunk_in")
        agg_ends_in = pair_of(sem, "agg_ends_in")
        kept_got = pair_of(sem, "kept_got")
        idx2_in = pair_of(sem, "idx2_in")
        rows2_in = pair_of(sem, "rows2_in")
        adds0_done = sem("adds0_done")
        adds1_done = sem("adds1_done")
        added1 = pair_of(sem, "added1")
        x_stored = pair_of(sem, "x_stored")
        last_in = pair_of(sem, "last_in")
        out_done = sem("out_done")
        out_stored = pair_of(sem, "out_stored")
        pool_set = sem("pool_set")
        vec_set = sem("vec_set")
        act_set = sem("act_set")
        pe_set = sem("pe_set")
        sp_steps = sem("sp_steps")
        pool_steps = sem("pool_steps")
        act_steps = sem("act_steps")
        pe_steps = sem("pe_steps")

        def hold(eng, steps, semaphore, value):
            eng.wait_ge(semaphore, value)
            eng.sem_inc(steps, 1)

        def ready(b):
            return b + 3

        def free1(b):
            return b + 2

        def free2(b):
            return b + 1

        def run(eng, block_body):
            with eng.Fori(0, LOOPS) as i:
                for s in range(2):
                    block_body(i, s)
            block_body(LOOPS, 0)

        def skewed(eng, turn):
            turn(0, 0, True, False, False)
            turn(0, 1, True, True, False)
            with eng.Fori(1, LOOPS) as i:
                turn(i, 0, True, True, True)
                turn(i, 1, True, True, True)
            turn(LOOPS, 0, True, True, True)
            turn(LOOPS, 1, False, True, True)
            turn(LOOPS + 1, 0, False, False, True)

        def place(t):
            return (t % 2) * 2 + t // 2

        def gate_rows(t):
            return (ps_m, ps_k[0])[t // 2][:, t % 2 * H:(t % 2 + 1) * H]

        blk = ctx.enter_context(nc.Block())

        @blk.sync
        def _(sp):
            def bc(a, n):
                return a.rearrange("(o n) -> o n", o=1).to_broadcast([P, n])

            def flat(a):
                return a.rearrange("o p w -> (o p) w")

            def stage1_early(i, s):
                b = i * 2 + s
                hold(sp, sp_steps, S["h1_done"], free2(b))
                sp.dma_start(feat[s][:, :], edge_feat[bass.ds(b, 1)].rearrange("o f e -> (o f) e")).then_inc(feat_in[s], 16)
                hold(sp, sp_steps, S["stats_done"], free2(b))
                hold(sp, sp_steps, S["same_done"], free2(b))
                hold(sp, sp_steps, S["once_done"], free2(b))
                sp.dma_start(idx[s][:, :], flat(edge_idx[bass.ds(b, 1)])).then_inc(idx_in[s], 16)
                sp.dma_start(rows[s][:, :], edge_rows[bass.ds(b, 1), BE:2 * BE].to_broadcast([P, BE])).then_inc(rows_in[s], 16)

            def stage1_late(i, s):
                b = i * 2 + s
                hold(sp, sp_steps, S["msg_done"], free2(b))
                hold(sp, sp_steps, S["hid_done"], free2(b))
                sp.dma_start(nodes[s][:, 2 * TILES:G1, :].rearrange("p r w -> p (r w)"),
                             flat(table_chunks[bass.ds(b, 1)])).then_inc(chunk_in[s], 16)

            def stage1_store(i, s):
                b = i * 2 + s
                sp.dma_start(flat(agg1_chunks[bass.ds(b, 1)]), bias_rows[:, :, :].rearrange("p r w -> p (r w)")).then_inc(agg1_set, 16)
                hold(sp, sp_steps, S["kept_done"], ready(b))
                sp.dma_start(flat(kept[bass.ds(b, 1)]), kept_out[s][:, :, :].rearrange("p r w -> p (r w)")).then_inc(kept_stored[s], 16)

            sp.dma_start(adaptt_sb[:, :], adaptt).then_inc(consts_in, 16)
            sp.dma_start(embt_sb[:, :], embt).then_inc(consts_in, 16)
            sp.dma_start(dist_sb[:, :], dist).then_inc(consts_in, 16)
            sp.dma_start(w1t_sb[:, :], w1t).then_inc(consts_in, 16)
            for h in (0, HALF):
                sp.dma_start(b1_sb[h:h + H, :], b1.rearrange("(n o) -> n o", o=1)).then_inc(consts_in, 16)
                sp.dma_start(w2b_sb[h:h + H + 1, :], w2b).then_inc(consts_in, 16)
            sp.dma_start(gamma_b[:, :], bc(gamma, H)).then_inc(consts_in, 16)
            sp.dma_start(beta_b[:, :], bc(beta, H)).then_inc(consts_in, 16)
            sp.dma_start(rb2_b[:, :], bc(rb2, H)).then_inc(consts_in, 16)
            sp.dma_start(norm_all[:, :], norm).then_inc(consts_in, 16)
            sp.dma_start(rel_all[:, :], rel).then_inc(consts_in, 16)
            sp.wait_ge(vec_set, 3)
            for s in range(2):
                stage1_early(0, s)
                stage1_late(0, s)
            with sp.Fori(0, LOOPS - 1) as i:
                for s in range(2):
                    stage1_early(i + 1, s)
                    stage1_late(i + 1, s)
                    stage1_store(i, s)
            stage1_early(LOOPS, 0)
            stage1_late(LOOPS, 0)
            stage1_store(LOOPS - 1, 0)
            stage1_store(LOOPS - 1, 1)
            stage1_store(LOOPS, 0)

            sp.wait_ge(kept_stored[0], 16 * (LOOPS + 1))
            sp.wait_ge(kept_stored[1], 16 * LOOPS)
            sp.wait_ge(added0[0], ADDS * (LOOPS + 1))
            sp.wait_ge(added0[1], ADDS * LOOPS)

            def stage2_idx(i, s):
                b = i * 2 + s
                hold(sp, sp_steps, S["tot_done"], free2(b))
                sp.dma_start(idx[s][:, :], flat(edge_idx[bass.ds(b, 1)])).then_inc(idx2_in[s], 16)

            def stage2_rows(i, s):
                b = i * 2 + s
                hold(sp, sp_steps, S["same1_done"], free2(b))
                hold(sp, sp_steps, S["once1_done"], free2(b))
                sp.dma_start(rows[s][:, :], edge_rows[bass.ds(b, 1), 0:BE].to_broadcast([P, BE])).then_inc(rows2_in[s], 16)
                sp.dma_start(dkey[s][:, :], flat(edge_idx[bass.ds(b, 1), :, 0:TILES])).then_inc(rows2_in[s], 16)

            def stage2_chunk(i, s, first):
                b = i * 2 + s
                hold(sp, sp_steps, S["x2_done"], free2(b))
                if not first:
                    hold(sp, sp_steps, x_stored[s], i * 16)
                sp.dma_start(agg_in[s][:, TILES:G2, :].rearrange("p r w -> p (r w)"),
                             flat(agg0_chunks[bass.ds(b, 1)])).then_inc(agg_chunk_in[s], 16)
                sp.dma_start(kept_in[s][:, :, :].rearrange("p r w -> p (r w)"), flat(kept[bass.ds(b, 1)])).then_inc(kept_got[s], 16)

            def stage2_store(i, s):
                b = i * 2 + s
                hold(sp, sp_steps, S["x2_done"], ready(b))
                sp.dma_start(flat(x_mid[bass.ds(b, 1)]), x2[s][:, TILES:G2, :].rearrange("p r w -> p (r w)")).then_inc(x_stored[s], 16)

            for s in range(2):
                stage2_idx(0, s)
                stage2_chunk(0, s, True)
            with sp.Fori(0, LOOPS - 1) as i:
                for s in range(2):
                    stage2_idx(i + 1, s)
                    stage2_rows(i, s)
                    stage2_store(i, s)
                    stage2_chunk(i + 1, s, False)
            stage2_idx(LOOPS, 0)
            stage2_rows(LOOPS - 1, 0)
            stage2_store(LOOPS - 1, 0)
            stage2_chunk(LOOPS, 0, False)
            stage2_rows(LOOPS - 1, 1)
            stage2_store(LOOPS - 1, 1)
            stage2_rows(LOOPS, 0)
            stage2_store(LOOPS, 0)

            sp.wait_ge(x_stored[0], 16 * (LOOPS + 1))
            sp.wait_ge(x_stored[1], 16 * LOOPS)
            sp.wait_ge(added1[0], ADDS * (LOOPS + 1))
            sp.wait_ge(added1[1], ADDS * LOOPS)

            def stage3_loads(i, s, first):
                b = i * 2 + s
                if not first:
                    hold(sp, sp_steps, out_done, free2(b))
                    hold(sp, sp_steps, out_stored[s], i * 16)
                sp.dma_start(agg_last[s][:, :], flat(agg1_chunks[bass.ds(b, 1)])).then_inc(last_in[s], 16)
                sp.dma_start(x_last[s][:, :], flat(x_mid[bass.ds(b, 1)])).then_inc(last_in[s], 16)

            stage3_loads(0, 0, True)
            stage3_loads(0, 1, True)
            with sp.Fori(1, LOOPS) as i:
                stage3_loads(i, 0, False)
                stage3_loads(i, 1, False)
            stage3_loads(LOOPS, 0, False)
            sp.wait_ge(out_stored[0], 16 * (LOOPS + 1))
            sp.wait_ge(out_stored[1], 16 * LOOPS)

        @blk.gpsimd
        def _(pool):
            nc.gpsimd.memset(zeros[:, :], 0.0).then_inc(pool_set, 1)
            nc.gpsimd.memset(ident[:, :], 0.0).then_inc(pool_set, 1)
            nc.gpsimd.memset(earlier[:, :], 1.0).then_inc(pool_set, 1)
            nc.gpsimd.memset(rw1_sb[:, :], OFF).then_inc(pool_set, 1)
            nc.gpsimd.memset(gate_in[:, :], 1.0).then_inc(pool_set, 1)
            nc.gpsimd.memset(rw2_sb[:, :, :], 0.0).then_inc(pool_set, 1)
            nc.gpsimd.memset(half_pi[:, :], float(np.pi / 2)).then_inc(pool_set, 1)
            nc.gpsimd.memset(eps[:, :], EPS).then_inc(pool_set, 1)
            nc.gpsimd.iota(iota_type[:, :], pattern=[[1, NTYPE]], base=0, channel_multiplier=0,
                           allow_small_or_imprecise_dtypes=True).then_inc(pool_set, 1)
            nc.gpsimd.iota(iota_rel[:, :], pattern=[[1, NREL]], base=0, channel_multiplier=0,
                           allow_small_or_imprecise_dtypes=True).then_inc(pool_set, 1)
            nc.gpsimd.iota(dump_id[:, :, :], pattern=[[0, TILES // 2], [P, 2]], base=DUMP, channel_multiplier=1,
                           allow_small_or_imprecise_dtypes=True).then_inc(pool_set, 1)
            pool.wait_ge(pool_set, 11)
            nc.gpsimd.affine_select(out=ident[:, :], in_=ident[:, :], compare_op=ALU.not_equal, fill=1.0, base=0,
                                    pattern=[[-1, P]], channel_multiplier=1).then_inc(pool_set, 1)
            nc.gpsimd.affine_select(out=earlier[:, P:2 * P], in_=earlier[:, P:2 * P], compare_op=ALU.is_gt, fill=0.0,
                                    base=0, pattern=[[-1, P]], channel_multiplier=1).then_inc(pool_set, 1)
            pool.sem_inc(adds0_done, 2)
            pool.sem_inc(adds1_done, 2)

            def nothing():
                pass

            def was_added0(i, s):
                hold(pool, adds0_done, added0[s], (i + 1) * ADDS)

            def was_added1(i, s):
                hold(pool, adds1_done, added1[s], (i + 1) * ADDS)

            def gather_ends(i, s, amid):
                b = i * 2 + s
                hold(pool, pool_steps, idx_in[s], (i + 1) * 16)
                hold(pool, pool_steps, S["hid_done"], free2(b))
                hold(pool, pool_steps, S["msg_done"], free2(b))
                for t in range(2 * TILES):
                    if t == TILES:
                        amid()
                    pool.indirect_dma_start(nodes[s][:, t, :], None, table,
                                            bass.IndirectOffsetOnAxis(ap=idx[s][:, t:t + 1], axis=0)).then_inc(ends_in[s], 16)

            def add0(i, s):
                b = i * 2 + s
                hold(pool, pool_steps, S["once_done"], ready(b))
                hold(pool, pool_steps, S["sums_copied"], ready(b))
                for q in range(TILES // 2):
                    if q:
                        hold(pool, pool_steps, added0[s], i * ADDS + 32 * q)
                    for t in (2 * q, 2 * q + 1):
                        pool.indirect_dma_start(agg0, bass.IndirectOffsetOnAxis(ap=once[s][:, t:t + 1], axis=0),
                                                sums[s][:, t, :], None, compute_op=ALU.add).then_inc(added0[s], 16)

            gather_ends(0, 0, nothing)
            gather_ends(0, 1, nothing)
            gather_ends(1, 0, nothing)
            pool.wait_ge(agg0_set, 16 * NBLOCK)
            add0(0, 0)
            with pool.Fori(1, LOOPS) as i:
                gather_ends(i, 1, lambda: was_added0(i - 1, 0))
                add0(i - 1, 1)
                gather_ends(i + 1, 0, lambda: was_added0(i - 1, 1))
                add0(i, 0)
            was_added0(LOOPS - 1, 0)
            add0(LOOPS - 1, 1)
            was_added0(LOOPS - 1, 1)
            add0(LOOPS, 0)
            pool.wait_ge(added0[0], ADDS * (LOOPS + 1))

            def gather_agg0(i, s, amid):
                b = i * 2 + s
                hold(pool, pool_steps, idx2_in[s], (i + 1) * 16)
                hold(pool, pool_steps, S["ydiv_done"], free2(b))
                for t in range(TILES):
                    if t == TILES // 2:
                        amid()
                    pool.indirect_dma_start(agg_in[s][:, t, :], None, agg0,
                                            bass.IndirectOffsetOnAxis(ap=idx[s][:, TILES + t:TILES + t + 1], axis=0)).then_inc(agg_ends_in[s], 16)

            def add1(i, s):
                b = i * 2 + s
                hold(pool, pool_steps, S["once1_done"], ready(b))
                hold(pool, pool_steps, S["sums1_copied"], ready(b))
                for q in range(TILES // 2):
                    if q:
                        hold(pool, pool_steps, added1[s], i * ADDS + 32 * q)
                    for t in (2 * q, 2 * q + 1):
                        pool.indirect_dma_start(agg1, bass.IndirectOffsetOnAxis(ap=once1[s][:, t:t + 1], axis=0),
                                                sums1[s][:, t, :], None, compute_op=ALU.add).then_inc(added1[s], 16)

            gather_agg0(0, 0, nothing)
            gather_agg0(0, 1, nothing)
            gather_agg0(1, 0, nothing)
            gather_agg0(1, 1, nothing)
            pool.wait_ge(agg1_set, 16 * NBLOCK)
            add1(0, 0)
            with pool.Fori(1, LOOPS - 1) as i:
                gather_agg0(i + 1, 0, lambda: was_added1(i - 1, 0))
                add1(i - 1, 1)
                gather_agg0(i + 1, 1, lambda: was_added1(i - 1, 1))
                add1(i, 0)
            gather_agg0(LOOPS, 0, lambda: was_added1(LOOPS - 2, 0))
            add1(LOOPS - 2, 1)
            was_added1(LOOPS - 2, 1)
            add1(LOOPS - 1, 0)
            was_added1(LOOPS - 1, 0)
            add1(LOOPS - 1, 1)
            was_added1(LOOPS - 1, 1)
            add1(LOOPS, 0)
            pool.wait_ge(added1[0], ADDS * (LOOPS + 1))

        @blk.tensor
        def _(pe):
            for n in ("onehot_t_done", "q_done", "h1_done", "gate_done", "sums_done",
                      "h2t_done", "k0_done", "k1_done", "k2_done", "m1_done", "m1t_done", "sums1_done"):
                pe.sem_inc(S[n], 2)
            pe.wait_ge(consts_in, CONSTS)
            nc.tensor.matmul(ps_t[0:GEMB, 0:NTYPE], adaptt_sb[:, :], embt_sb[:, :], start=True, stop=True).then_inc(pe_set, 1)
            pe.wait_ge(vec_set, 1)
            nc.tensor.matmul(ps_q[0:NTYPE, 0:NTYPE], embt_sb[:, :], ada[:, :], start=True, stop=True).then_inc(pe_set, 1)
            pe.wait_ge(pool_set, 13)
            pe.wait_ge(vec_set, 2)

            def h1(i, s):
                b = i * 2 + s
                hold(pe, pe_steps, feat_in[s], (i + 1) * 16)
                hold(pe, pe_steps, S["gate_in_done"], free1(b))
                for h in range(2):
                    last = nc.tensor.matmul(ps_h[HALF * h:HALF * h + H, 0:BE // 2], w1t_sb[:, :],
                                            feat[s][:, h * (BE // 2):(h + 1) * (BE // 2)], start=True, stop=True)
                last.then_inc(S["h1_done"], 1)

            def sums_of_pairs(s, width, m, at):
                for q in range(TILES // 2):
                    a = 2 * q
                    nc.tensor.matmul(ps_s[:, a * width:(a + 1) * width], same_a[s][:, q, :], m[:, at(a), :], start=True, stop=False)
                    nc.tensor.matmul(ps_s[:, a * width:(a + 1) * width], same_b[s][:, q, 0:P], m[:, at(a + 1), :], start=False, stop=True)
                    last = nc.tensor.matmul(ps_s[:, (a + 1) * width:(a + 2) * width], same_b[s][:, q, P:2 * P], m[:, at(a + 1), :],
                                            start=True, stop=True)
                return last

            def stage1(i, s, more):
                b = i * 2 + s
                hold(pe, pe_steps, S["onehot_done"], ready(b))
                hold(pe, pe_steps, S["onehot_copied"], free1(b))
                for t in range(TILES):
                    last = nc.tensor.transpose(ps_t[0:NTYPE, t * P:(t + 1) * P], onehot[:, t, :], ident[:, :])
                last.then_inc(S["onehot_t_done"], 1)
                hold(pe, pe_steps, S["gate_in_done"], ready(b))
                hold(pe, pe_steps, S["msg_done"], free1(b))
                for t in range(TILES):
                    h = HALF * (t // 2)
                    last = nc.tensor.matmul(gate_rows(t), gate_in[h:h + H + 1, t % 2 * P:(t % 2 + 1) * P],
                                            w2b_sb[h:h + H + 1, :], start=True, stop=True)
                last.then_inc(S["gate_done"], 1)
                hold(pe, pe_steps, S["onehot_copied"], ready(b))
                hold(pe, pe_steps, S["logit_done"], free1(b))
                for t in range(TILES):
                    last = nc.tensor.matmul(ps_q[:, t * NTYPE:(t + 1) * NTYPE], onehot_t[:, t, :], q_sb[:, :], start=True, stop=True)
                last.then_inc(S["q_done"], 1)
                if more:
                    h1(i + s, 1 - s)
                hold(pe, pe_steps, S["same_done"], ready(b))
                hold(pe, pe_steps, S["msg_done"], ready(b))
                hold(pe, pe_steps, S["sums_copied"], free1(b))
                sums_of_pairs(s, AW, msg, lambda t: t).then_inc(S["sums_done"], 1)

            h1(0, 0)
            with pe.Fori(0, LOOPS) as i:
                stage1(i, 0, True)
                stage1(i, 1, True)
            stage1(LOOPS, 0, False)
            pe.wait_ge(rw1_in, 32)
            pe.wait_ge(rb1_in, 16 * NREL)

            def stage2(i, s, y, e, d):
                b = i * 2 + s
                if e:
                    hold(pe, pe_steps, S["rel_done"], ready(b - 1))
                    hold(pe, pe_steps, S["h2_done"], ready(b - 1))
                    hold(pe, pe_steps, S["h2t_copied"], free1(b - 1))
                    for t in range(TILES):
                        last = nc.tensor.transpose(ps_t[0:H + NREL, t * P:(t + 1) * P], h2[:, t, :], ident[:, :])
                    last.then_inc(S["h2t_done"], 1)
                if d:
                    hold(pe, pe_steps, S["same1_done"], ready(b - 2))
                    hold(pe, pe_steps, S["msg1_done"], ready(b - 2))
                    hold(pe, pe_steps, S["sums1_copied"], free1(b - 2))
                    sums_of_pairs(s, H, msg1, place).then_inc(S["sums1_done"], 1)
                if e:
                    hold(pe, pe_steps, S["h2t_copied"], ready(b - 1))
                    for k in range(KC):
                        hold(pe, pe_steps, S[f"relu{k}_done"], free1(b - 1))
                        nc.tensor.matmul(ps_k[k][:, :], rw1_sb[:, k * P:(k + 1) * P], h2_t[:, :],
                                         start=True, stop=True).then_inc(S[f"k{k}_done"], 1)
                    hold(pe, pe_steps, S["m1_copied"], free1(b - 1))
                    for k in range(KC):
                        hold(pe, pe_steps, S[f"relu{k}_done"], ready(b - 1))
                        for h in range(2):
                            last = nc.tensor.matmul(ps_m[HALF * h:HALF * (h + 1), 0:BE // 2], rw2_sb[:, k, :],
                                                    hid1[:, k, h * (BE // 2):(h + 1) * (BE // 2)], start=(k == 0), stop=(k == KC - 1))
                    last.then_inc(S["m1_done"], 1)
                    hold(pe, pe_steps, S["m1_copied"], ready(b - 1))
                    hold(pe, pe_steps, S["msg1_done"], free1(b - 1))
                    for t in range(TILES // 2):
                        last = nc.tensor.transpose(ps_q[:, t * P:(t + 1) * P], msg1_t[:, t * P:(t + 1) * P], ident[:, :])
                    last.then_inc(S["m1t_done"], 1)

            skewed(pe, stage2)

        @blk.scalar
        def _(act):
            for n in ("onehot_copied", "gate_in_done", "std_done", "hid_dst_done", "hid_done", "sums_copied", "ysq_done",
                      "ystd_done", "esq_done", "estd_done", "h2_done", "h2t_copied", "relu0_done", "relu1_done",
                      "relu2_done", "m1_copied", "sums1_copied"):
                act.sem_inc(S[n], 2)
            act.wait_ge(pool_set, 11)
            with act.Fori(0, NBLOCK) as c:
                act.dma_start(agg0_chunks[bass.ds(c, 1)].rearrange("o p w -> (o p) w"), zeros[:, :]).then_inc(agg0_set, 16)
            act.dma_start(rw1_sb[0:H, :], rw1).then_inc(rw1_in, 16)
            act.dma_start(rw2_sb[:, :, 0:H], rw2.rearrange("(k p) h -> p k h", p=P)).then_inc(rw1_in, 16)
            for r in range(NREL):
                act.dma_start(rw1_sb[H + r:H + r + 1, r * H:(r + 1) * H], rb1.rearrange("(o n) -> o n", o=1)).then_inc(rb1_in, 16)
            act.wait_ge(vec_set, 4)
            nc.scalar.activation(cw_b[:, :], cw_a[:, :], ACT.Sin, bias=half_pi[:, :], scale=-float(np.pi) / CUTOFF).then_inc(act_set, 1)

            def gate_hidden(i, s):
                b = i * 2 + s
                hold(act, act_steps, S["h1_done"], ready(b))
                hold(act, act_steps, S["gate_done"], free1(b))
                for h in (0, HALF):
                    last = nc.scalar.activation(gate_in[h:h + H, :], ps_h[h:h + H, 0:BE // 2], ACT.Silu,
                                                bias=b1_sb[h:h + H, :], scale=1.0)
                last.then_inc(S["gate_in_done"], 1)

            def stage1(i, s, more):
                b = i * 2 + s
                hold(act, act_steps, S["onehot_t_done"], ready(b))
                hold(act, act_steps, S["q_done"], free1(b))
                nc.scalar.copy(onehot_t[:, :, :].rearrange("p t e -> p (t e)"), ps_t[0:NTYPE, :]).then_inc(S["onehot_copied"], 1)
                hold(act, act_steps, S["var_done"], ready(b))
                hold(act, act_steps, S["rstd_done"], free1(b))
                nc.scalar.activation(std[:, :], var[:, :], ACT.Sqrt, bias=eps[:, :], scale=1.0 / H).then_inc(S["std_done"], 1)
                hold(act, act_steps, S["kept_done"], free2(b))
                hold(act, act_steps, S["shift_done"], ready(b))
                for r in range(G1):
                    row = nc.scalar.activation(hid[s][:, r, :], nodes[s][:, r, 0:H], ACT.Relu, bias=shift[:, r:r + 1],
                                               scale=rstd[:, r:r + 1],
                                               **({} if r < TILES else {"accum_out": hsum[s][:, r - TILES:r - TILES + 1]}))
                    if r == TILES - 1:
                        row.then_inc(S["hid_dst_done"], 1)
                row.then_inc(S["hid_done"], 1)
                if more:
                    gate_hidden(i + s, 1 - s)
                hold(act, act_steps, adds0_done, free2(b))
                hold(act, act_steps, S["sums_done"], ready(b))
                nc.scalar.copy(sums[s][:, :, :].rearrange("p t w -> p (t w)"), ps_s[:, 0:TILES * AW]).then_inc(S["sums_copied"], 1)

            act.wait_ge(consts_in, CONSTS)
            gate_hidden(0, 0)
            with act.Fori(0, LOOPS) as i:
                stage1(i, 0, True)
                stage1(i, 1, True)
            stage1(LOOPS, 0, False)

            def stage2(i, s, y, e, d):
                b = i * 2 + s
                if e:
                    hold(act, act_steps, S["ecen_done"], ready(b - 1))
                    hold(act, act_steps, S["evar_done"], free1(b - 1))
                    nc.scalar.activation(sq[:, :, :], cen[:, :, :], ACT.Square).then_inc(S["esq_done"], 1)
                if y:
                    hold(act, act_steps, S["ycen_done"], ready(b))
                    hold(act, act_steps, S["yvar_done"], free1(b))
                    nc.scalar.activation(ysq[:, :, :], ycen2[:, :, :], ACT.Square).then_inc(S["ysq_done"], 1)
                if e:
                    hold(act, act_steps, S["evar_done"], ready(b - 1))
                    hold(act, act_steps, S["erstd_done"], free1(b - 1))
                    nc.scalar.activation(estd[:, :], evar[:, :], ACT.Sqrt, bias=eps[:, :], scale=1.0 / H).then_inc(S["estd_done"], 1)
                if y:
                    hold(act, act_steps, S["yvar_done"], ready(b))
                    hold(act, act_steps, S["yrstd_done"], free1(b))
                    nc.scalar.activation(ystd[:, :], yvar[:, :], ACT.Sqrt, bias=eps[:, :], scale=1.0 / H).then_inc(S["ystd_done"], 1)
                if e:
                    hold(act, act_steps, S["enrm_done"], ready(b - 1))
                    hold(act, act_steps, S["h2t_done"], free1(b - 1))
                    nc.scalar.activation(h2[:, :, 0:H], h2n[:, :, :], ACT.Relu).then_inc(S["h2_done"], 1)
                if e:
                    hold(act, act_steps, S["h2t_done"], ready(b - 1))
                    hold(act, act_steps, S["k2_done"], free1(b - 1))
                    nc.scalar.copy(h2_t[:, :], ps_t[0:H + NREL, :]).then_inc(S["h2t_copied"], 1)
                if d:
                    hold(act, act_steps, adds1_done, free2(b - 2))
                    hold(act, act_steps, S["sums1_done"], ready(b - 2))
                    nc.scalar.copy(sums1[s][:, :, :].rearrange("p t w -> p (t w)"), ps_s[:, 0:TILES * H]).then_inc(S["sums1_copied"], 1)
                if e:
                    hold(act, act_steps, S["m1_done"], free1(b - 1))
                    for k in range(KC):
                        hold(act, act_steps, S[f"k{k}_done"], ready(b - 1))
                        nc.scalar.activation(hid1[:, k, :], ps_k[k][:, :], ACT.Relu).then_inc(S[f"relu{k}_done"], 1)
                    hold(act, act_steps, S["m1_done"], ready(b - 1))
                    hold(act, act_steps, S["m1t_done"], free1(b - 1))
                    nc.scalar.copy(msg1_t[:, :], ps_m[:, 0:BE // 2]).then_inc(S["m1_copied"], 1)

            skewed(act, stage2)

            def stage3(i, s):
                b = i * 2 + s
                hold(act, act_steps, out_done, ready(b))
                act.dma_start(out_chunks[bass.ds(b, 1)].rearrange("o p w -> (o p) w"), out_sb[s][:, :]).then_inc(out_stored[s], 16)

            run(act, stage3)

        @blk.vector
        def _(dve):
            for n in ("stats_done mean2_done mdiff_done vsum_done vmix_done var_done rstd_done shift_done hmean_done kept_done "
                      "ahead_done turn_done turned_done once_done same_done onehot_done logit_done coef_done hdst_done "
                      "raw_done mmean_done msg_done tot_done rtot_done ydiv_done ycen_done yvar_done yrstd_done "
                      "ynrm_done ygam_done x2_done esum_done emean_done ecen_done evar_done erstd_done enrm_done "
                      "rel_done msg1_done same1_done ahead1_done turn1_done turned1_done once1_done").split():
                dve.sem_inc(S[n], 2)
            dve.sem_inc(out_done, 2)

            V = nc.vector

            def cols(a, n):
                return a.unsqueeze(2).to_broadcast([P, a.shape[1], n])

            def each(a, n):
                return a.unsqueeze(1).to_broadcast([P, n, a.shape[1]])

            dve.wait_ge(consts_in, CONSTS)
            dve.wait_ge(pe_set, 1)
            V.tensor_copy(ada[:, :], ps_t[0:GEMB, 0:NTYPE]).then_inc(vec_set, 1)
            dve.wait_ge(pe_set, 2)
            V.tensor_copy(q_sb[:, :], ps_q[0:NTYPE, 0:NTYPE]).then_inc(vec_set, 1)
            V.tensor_copy(bias_rows[:, :, :], each(rb2_b[:, :], NR)).then_inc(vec_set, 1)
            V.tensor_scalar(cw_all[:, :], dist_sb[:, :], -1.0, CUTOFF, ALU.mult, ALU.min).then_inc(act_set, 1)
            V.tensor_scalar(cw_b[:, :], dist_sb[:, :], CUTOFF, None, ALU.min).then_inc(act_set, 1)
            dve.wait_ge(act_set, 2)
            V.tensor_tensor(cw_a[:, :], cw_all[:, :], cw_b[:, :], ALU.max).then_inc(vec_set, 1)
            dve.wait_ge(act_set, 3)
            V.tensor_scalar(cw_a[:, :], cw_b[:, :], 1.0, 0.5, ALU.add, ALU.mult).then_inc(act_set, 1)
            dve.wait_ge(act_set, 4)
            V.scalar_tensor_tensor(out=cw_all[:, :], in0=dist_sb[:, :], scalar=CUTOFF, in1=cw_a[:, :],
                                   op0=ALU.is_lt, op1=ALU.mult).then_inc(act_set, 1)
            dve.wait_ge(act_set, 5)
            dve.wait_ge(pool_set, 13)

            def same_node(s, keys):
                for q in range(TILES // 2):
                    a = 2 * q
                    V.tensor_scalar(same_a[s][:, q, :], rows[s][:, a * P:(a + 1) * P], keys[:, a:a + 1], None, ALU.is_equal)
                    last = V.tensor_scalar(same_b[s][:, q, :], rows[s][:, a * P:(a + 2) * P],
                                           keys[:, a + 1:a + 2], None, ALU.is_equal)
                return last

            def count_ahead(s, keys, work, counts):
                for t in range(TILES):
                    a = t - t % 2
                    n = P * (1 + t % 2)
                    last = V.scalar_tensor_tensor(out=work[:, t, 0:n], in0=rows[s][:, a * P:a * P + n], scalar=keys[:, t:t + 1],
                                                  in1=earlier[:, 2 * P - n:2 * P], op0=ALU.is_equal, op1=ALU.mult,
                                                  accum_out=counts[:, t:t + 1])
                return last

            dump = dump_id[:, :, :].rearrange("p q a -> p (q a)")

            def keep_hidden(i, s):
                b = i * 2 + s
                dve.wait_ge(S["hid_done"], ready(b))
                V.tensor_scalar(hmean[:, :], hsum[s][:, :], -1.0 / H, None, ALU.mult).then_inc(S["hmean_done"], 1)
                dve.wait_ge(S["hmean_done"], ready(b))
                V.tensor_tensor(kept_out[s][:, :, 0:H], hid[s][:, TILES:G1, :], cols(hmean[:, :], H), ALU.add).then_inc(S["kept_done"], 1)

            def stage1(i, s, behind, first):
                b = i * 2 + s
                keys = idx[s][:, TILES:2 * TILES]
                dve.wait_ge(ends_in[s], (i + 1) * (2 * TILES * 16))
                dve.wait_ge(chunk_in[s], (i + 1) * 16)
                dve.wait_ge(S["onehot_t_done"], free1(b))
                V.tensor_tensor(onehot[:, :, :], each(iota_type[:, :], TILES),
                                nodes[s][:, TILES:2 * TILES, H + 1:H + 2].bitcast(I32).to_broadcast([P, TILES, NTYPE]),
                                ALU.is_equal).then_inc(S["onehot_done"], 1)
                for r in range(G1):
                    last = V.bn_stats(stats[:, r, :], nodes[s][:, r, 0:H])
                last.then_inc(S["stats_done"], 1)
                dve.wait_ge(S["stats_done"], ready(b))

                def of(n):
                    return stats[:, :, n:n + 1].rearrange("p r o -> p (r o)")

                V.tensor_tensor(mdiff[:, :], of(1), of(4), ALU.subtract).then_inc(S["mdiff_done"], 1)
                V.tensor_tensor(vsum[:, :], of(2), of(5), ALU.add).then_inc(S["vsum_done"], 1)
                V.tensor_tensor(mean2[:, :], of(1), of(4), ALU.add).then_inc(S["mean2_done"], 1)
                dve.wait_ge(S["mdiff_done"], ready(b))
                V.scalar_tensor_tensor(out=vmix[:, :], in0=mdiff[:, :], scalar=H / 4.0, in1=mdiff[:, :], op0=ALU.mult,
                                       op1=ALU.mult).then_inc(S["vmix_done"], 1)
                dve.wait_ge(rows_in[s], (i + 1) * 16)
                dve.wait_ge(idx_in[s], (i + 1) * 16)
                V.tensor_tensor(turn[:, :], dump, keys, ALU.subtract).then_inc(S["turn_done"], 1)
                dve.wait_ge(S["vmix_done"], ready(b))
                V.tensor_tensor(var[:, :], vsum[:, :], vmix[:, :], ALU.add).then_inc(S["var_done"], 1)
                count_ahead(s, keys, junk, ahead).then_inc(S["ahead_done"], 1)
                if behind:
                    keep_hidden(i + s - 1, 1 - s)
                dve.wait_ge(S["std_done"], ready(b))
                V.reciprocal(rstd[:, :], std[:, :]).then_inc(S["rstd_done"], 1)
                dve.wait_ge(S["rstd_done"], ready(b))
                V.scalar_tensor_tensor(out=shift[:, :], in0=mean2[:, :], scalar=-0.5, in1=rstd[:, :], op0=ALU.mult,
                                       op1=ALU.mult).then_inc(S["shift_done"], 1)
                dve.wait_ge(S["ahead_done"], ready(b))
                V.scalar_tensor_tensor(out=turned[:, :], in0=ahead[:, :], scalar=0.0, in1=turn[:, :], op0=ALU.is_gt,
                                       op1=ALU.mult).then_inc(S["turned_done"], 1)
                same_node(s, keys).then_inc(S["same_done"], 1)
                dve.wait_ge(S["turned_done"], ready(b))
                dve.wait_ge(adds0_done, free2(b))
                V.tensor_tensor(once[s][:, :], keys, turned[:, :], ALU.add).then_inc(S["once_done"], 1)
                node_w = nodes[s][:, 0:TILES, H:H + 1].rearrange("p t o -> p (t o)")
                V.tensor_tensor(coef[:, :], node_w, cw_all[:, bass.ds(b * TILES, TILES)], ALU.mult).then_inc(S["coef_done"], 1)
                dve.wait_ge(S["q_done"], ready(b))
                for t in range(TILES):
                    last = V.scalar_tensor_tensor(out=junk_q[:, t, :], in0=iota_type[:, :],
                                                  scalar=nodes[s][:, t, H + 1:H + 2].bitcast(I32),
                                                  in1=ps_q[:, t * NTYPE:(t + 1) * NTYPE], op0=ALU.is_equal, op1=ALU.mult,
                                                  accum_out=logit[:, t:t + 1])
                last.then_inc(S["logit_done"], 1)
                dve.wait_ge(S["coef_done"], ready(b))
                dve.wait_ge(S["hid_dst_done"], ready(b))
                V.tensor_tensor(hdst[:, :, :], hid[s][:, 0:TILES, :], cols(coef[:, :], H), ALU.mult).then_inc(S["hdst_done"], 1)
                dve.wait_ge(S["logit_done"], ready(b))
                dve.wait_ge(S["hdst_done"], ready(b))
                dve.wait_ge(S["gate_done"], ready(b))
                for t in range(TILES):
                    last = V.scalar_tensor_tensor(out=msg_raw[:, t, :], in0=gate_rows(t), scalar=logit[:, t:t + 1],
                                                  in1=hdst[:, t, :], op0=ALU.add, op1=ALU.mult, accum_out=msum[:, t:t + 1])
                last.then_inc(S["raw_done"], 1)
                if not first:
                    dve.wait_ge(kept_stored[s], i * 16)
                V.tensor_tensor(kept_out[s][:, :, H:HW], nodes[s][:, TILES:G1, 0:H], each(beta_b[:, :], G2), ALU.add)
                dve.wait_ge(S["raw_done"], ready(b))
                V.tensor_scalar(mmean[:, :], msum[:, :], -1.0 / H, None, ALU.mult).then_inc(S["mmean_done"], 1)
                dve.wait_ge(S["sums_done"], free1(b))
                V.tensor_copy(msg[:, :, H:AW], nodes[s][:, 0:TILES, H:H + 1])
                dve.wait_ge(S["mmean_done"], ready(b))
                V.tensor_tensor(msg[:, :, 0:H], msg_raw[:, :, :], cols(mmean[:, :], H), ALU.add).then_inc(S["msg_done"], 1)

            stage1(0, 0, False, True)
            stage1(0, 1, True, True)
            with dve.Fori(1, LOOPS) as i:
                stage1(i, 0, True, False)
                stage1(i, 1, True, False)
            stage1(LOOPS, 0, True, False)
            keep_hidden(LOOPS, 0)

            def stage2(i, s, y, e, d):
                b = i * 2 + s
                if y:
                    dve.wait_ge(agg_chunk_in[s], (i + 1) * 16)
                    dve.wait_ge(agg_ends_in[s], (i + 1) * (TILES * 16))
                    V.tensor_scalar(tot[:, :], agg_in[s][:, :, H:AW].rearrange("p r o -> p (r o)"), 1e-8, None, ALU.max).then_inc(S["tot_done"], 1)
                if e:
                    dve.wait_ge(S["x2_done"], ready(b - 1))
                    V.tensor_reduce(stat[:, :], x2[1 - s][:, 0:TILES, :], AX_X, ALU.add).then_inc(S["esum_done"], 1)
                if y:
                    dve.wait_ge(S["tot_done"], ready(b))
                    V.reciprocal(rtot[:, :], tot[:, :]).then_inc(S["rtot_done"], 1)
                if e:
                    dve.wait_ge(S["esum_done"], ready(b - 1))
                    V.tensor_scalar(nmean[:, :], stat[:, :], -1.0 / H, None, ALU.mult).then_inc(S["emean_done"], 1)
                if y:
                    dve.wait_ge(S["rtot_done"], ready(b))
                    V.tensor_tensor(ycen[:, :, :], agg_in[s][:, :, 0:H], cols(rtot[:, :], H), ALU.mult).then_inc(S["ydiv_done"], 1)
                if e:
                    dve.wait_ge(S["emean_done"], ready(b - 1))
                    V.tensor_tensor(cen[:, :, :], x2[1 - s][:, 0:TILES, :], cols(nmean[:, :], H), ALU.add).then_inc(S["ecen_done"], 1)
                    dve.wait_ge(S["h2t_done"], free1(b - 1))
                    V.tensor_tensor(h2[:, :, H:H + NREL], each(iota_rel[:, :], TILES),
                                    rel_all[:, bass.ds((b - 1) * TILES, TILES)].unsqueeze(2).to_broadcast([P, TILES, NREL]),
                                    ALU.is_equal).then_inc(S["rel_done"], 1)
                if y:
                    dve.wait_ge(S["ydiv_done"], ready(b))
                    dve.wait_ge(kept_got[s], (i + 1) * 16)
                    V.tensor_tensor(ycen2[:, :, :], ycen[:, :, :], kept_in[s][:, :, 0:H], ALU.add).then_inc(S["ycen_done"], 1)
                if e:
                    dve.wait_ge(S["esq_done"], ready(b - 1))
                    V.tensor_reduce(evar[:, :], sq[:, :, :], AX_X, ALU.add).then_inc(S["evar_done"], 1)
                if d:
                    dve.wait_ge(rows2_in[s], i * 32)
                    V.tensor_tensor(turn1[:, :], dump, dkey[s][:, :], ALU.subtract).then_inc(S["turn1_done"], 1)
                    same_node(s, dkey[s]).then_inc(S["same1_done"], 1)
                    count_ahead(s, dkey[s], junk1, ahead1).then_inc(S["ahead1_done"], 1)
                if y:
                    dve.wait_ge(S["ysq_done"], ready(b))
                    V.tensor_reduce(yvar[:, :], ysq[:, :, :], AX_X, ALU.add).then_inc(S["yvar_done"], 1)
                if e:
                    dve.wait_ge(S["estd_done"], ready(b - 1))
                    V.reciprocal(erstd[:, :], estd[:, :]).then_inc(S["erstd_done"], 1)
                if e:
                    dve.wait_ge(S["erstd_done"], ready(b - 1))
                    V.tensor_tensor(h2n[:, :, :], cen[:, :, :], cols(erstd[:, :], H), ALU.mult).then_inc(S["enrm_done"], 1)
                if d:
                    dve.wait_ge(S["m1t_done"], ready(b - 2))
                    dve.wait_ge(S["sums1_done"], free1(b - 2))
                    V.tensor_tensor(msg1[:, :, :], ps_q[:, 0:2 * P].rearrange("p (t h) -> p t h", t=TILES)[:, :, 0:H],
                                    cols(norm_all[:, bass.ds((b - 2) * TILES, TILES)], H), ALU.mult).then_inc(S["msg1_done"], 1)
                if d:
                    dve.wait_ge(S["ahead1_done"], ready(b - 2))
                    dve.wait_ge(S["turn1_done"], ready(b - 2))
                    V.scalar_tensor_tensor(out=turned1[:, :], in0=ahead1[:, :], scalar=0.0, in1=turn1[:, :], op0=ALU.is_gt,
                                           op1=ALU.mult).then_inc(S["turned1_done"], 1)
                if y:
                    dve.wait_ge(S["ystd_done"], ready(b))
                    V.reciprocal(yrstd[:, :], ystd[:, :]).then_inc(S["yrstd_done"], 1)
                if d:
                    dve.wait_ge(S["turned1_done"], ready(b - 2))
                    dve.wait_ge(adds1_done, free2(b - 2))
                    V.tensor_tensor(once1[s][:, :], dkey[s][:, :], turned1[:, :], ALU.add).then_inc(S["once1_done"], 1)
                if y:
                    dve.wait_ge(S["yrstd_done"], ready(b))
                    V.tensor_tensor(ynrm[:, :, :], ycen2[:, :, :], cols(yrstd[:, :], H), ALU.mult).then_inc(S["ynrm_done"], 1)
                    dve.wait_ge(S["ynrm_done"], ready(b))
                    V.tensor_tensor(ygam[:, :, :], ynrm[:, :, :], each(gamma_b[:, :], G2), ALU.mult).then_inc(S["ygam_done"], 1)
                    dve.wait_ge(S["ygam_done"], ready(b))
                    V.tensor_tensor(x2[s][:, :, :], ygam[:, :, :], kept_in[s][:, :, H:HW], ALU.add).then_inc(S["x2_done"], 1)

            skewed(dve, stage2)

            def stage3(i, s):
                dve.wait_ge(last_in[s], (i + 1) * 32)
                V.scalar_tensor_tensor(out=out_sb[s][:, :], in0=agg_last[s][:, :], scalar=0.0, in1=x_last[s][:, :],
                                       op0=ALU.max, op1=ALU.add).then_inc(out_done, 1)

            run(dve, stage3)


def kernel(**inputs):
    import concourse.bacc as bacc
    from concourse.bass_utils import run_bass_kernel_spmd

    a = {k: np.asarray(v) for k, v in inputs.items()}
    ep = NBLOCK * BE

    def edges(v, fill=0):
        full = np.full((ep,), fill, v.dtype)
        full[:E] = v.reshape(-1)
        return full.reshape(NBLOCK, TILES, P)

    def columns(v):
        return v.transpose(0, 2, 1)

    src, dst = edges(a["src"], NULL), edges(a["dst"], NULL)
    table = np.zeros((NP, TW), np.float32)
    table[:N, :H] = a["x"]
    table[:N, H] = a["node_vec"]
    table[:N, H + 1] = a["node_type_119"].astype(np.int32).view(np.float32)
    feat = np.zeros((ep, RAD), np.float32)
    feat[:E] = a["edge_attr_40"]
    arrays = {
        "table": table,
        "edge_idx": np.concatenate([columns(dst), columns(src)], 2),
        "edge_rows": np.concatenate([dst.reshape(NBLOCK, BE), src.reshape(NBLOCK, BE)], 1),
        "edge_feat": feat.reshape(NBLOCK, BE, RAD).transpose(0, 2, 1),
        "dist": columns(edges(a["edge_weight"])).transpose(1, 0, 2).reshape(P, NBLOCK * TILES),
        "norm": columns(edges(a["edge_weight1"]))[:, :, [0, 2, 1, 3]].transpose(1, 0, 2).reshape(P, NBLOCK * TILES),
        "rel": columns(edges(a["edge_type_8"])).transpose(1, 0, 2).reshape(P, NBLOCK * TILES),
        "w1t": a["L0_gnn_W1"].T,
        "b1": a["L0_gnn_b1"],
        "w2b": np.concatenate([a["L0_gnn_W2"].T, a["L0_gnn_b2"][None]], 0),
        "embt": a["L0_gnn_emb"].T,
        "adaptt": a["L0_gnn_adaptW"].T,
        "gamma": a["L0_gnn_gamma"],
        "beta": a["L0_gnn_beta"],
        "rw1": a["L1_gnn_weight1"].transpose(1, 0, 2).reshape(H, CW1),
        "rb1": a["L1_gnn_bias1"],
        "rw2": a["L1_gnn_weight2"].reshape(CW1, H),
        "rb2": a["L1_gnn_bias2"],
    }
    nc = bacc.Bacc("TRN2", target_bir_lowering=False, num_devices=1)
    given, aps = {}, []
    for name, v in arrays.items():
        v = np.ascontiguousarray(v)
        given[f"in_{name}"] = v
        aps.append(nc.dram_tensor(f"in_{name}", v.shape, mybir.dt.from_np(v.dtype), kind="ExternalInput").ap())
    out = nc.dram_tensor("out_0", (NP, H), F32, kind="ExternalOutput").ap()
    build(nc, *aps, out)
    r = run_bass_kernel_spmd(nc, [given], core_ids=[0])
    return r.results[0]["out_0"][:N]
```

```python
from contextlib import ExitStack

import concourse.bass as bass
from concourse import mybir
import numpy as np

F32 = mybir.dt.float32
I32 = mybir.dt.int32
ALU = mybir.AluOpType
ACT = mybir.ActivationFunctionType
CONSTS = 13 * 16
AX_X = mybir.AxisListType.X

P = 128
N = 100000
E = 25000
H = 48
RAD = 40
NREL = 8
NTYPE = 119
GEMB = 32
CUTOFF = 6.0
EPS = 1e-5

TILES = 4
BE = TILES * P
NBLOCK = -(-E // BE)
NR = 16
NP = NBLOCK * P * NR
NULL = N
DUMP = NP - 2 * P
assert NULL < DUMP and NP >= N
TW = H + 2
AW = H + 1
G1 = 2 * TILES + NR
G2 = TILES + NR
KW = (G2 + TILES) * H
CW1 = NREL * H
KC = CW1 // P
OFF = -1.0e30
ADDS = 16 * TILES
HALF = 64
SLOTS = 4
ROUNDS = NBLOCK // SLOTS
ZERO_SLOTS = 4
ZERO_ROUNDS = NBLOCK // ZERO_SLOTS
ZERO_1 = ZERO_ROUNDS * 2 // 5
ZERO_2 = ZERO_ROUNDS * 3 // 5
LOOPS = NBLOCK // 2
assert NBLOCK == 2 * LOOPS + 1 == SLOTS * ROUNDS + 1 and CW1 == KC * P


def build(nc, table, edge_idx, edge_rows, edge_feat, dist, norm, rel, w1t, b1, w2b, embt, adaptt,
          gamma, beta, rw1, rb1, rw2, rb2, out):
    agg0 = nc.dram_tensor("agg0", [NP, AW], F32).ap()
    agg1 = nc.dram_tensor("agg1", [NP, H], F32).ap()
    kept = nc.dram_tensor("kept", [NBLOCK, P, KW], F32).ap()
    x_mid = nc.dram_tensor("x_mid", [NBLOCK, P, NR * H], F32).ap()
    table_chunks = table.rearrange("(c p r) w -> c p (r w)", p=P, r=NR)
    agg0_chunks = agg0.rearrange("(c p r) w -> c p (r w)", p=P, r=NR)
    agg1_chunks = agg1.rearrange("(c p r) w -> c p (r w)", p=P, r=NR)
    out_chunks = out.rearrange("(c p r) w -> c p (r w)", p=P, r=NR)

    with ExitStack() as ctx:
        def sb(name, shape, dt=F32):
            return ctx.enter_context(nc.sbuf_tensor(name, shape, dt))

        def sem(name):
            return ctx.enter_context(nc.semaphore(name))

        def pair_of(make, name, *args):
            return [make(f"{name}_{s}", *args) for s in range(2)]

        def slots_of(make, name, *args):
            return [make(f"{name}_{s}", *args) for s in range(SLOTS)]

        ident = sb("ident", [P, P])
        iota_type = sb("iota_type", [P, NTYPE])
        iota_rel = sb("iota_rel", [P, NREL])
        earlier = sb("earlier", [P, 2 * P])
        dump_id = sb("dump_id", [P, TILES // 2, 2])
        zeros = sb("zeros", [P, NR * AW])
        bias_rows = sb("bias_rows", [P, NR, H])
        half_pi = sb("half_pi", [P, 1])
        eps = sb("eps", [P, 1])
        w1t_sb = sb("w1t_sb", [RAD, H])
        b1_sb = sb("b1_sb", [P, 1])
        w2b_sb = sb("w2b_sb", [P, H])
        embt_sb = sb("embt_sb", [GEMB, NTYPE])
        adaptt_sb = sb("adaptt_sb", [GEMB, GEMB])
        ada = sb("ada", [GEMB, NTYPE])
        q_sb = sb("q_sb", [NTYPE, NTYPE])
        gamma_b = sb("gamma_b", [P, H])
        beta_b = sb("beta_b", [P, H])
        rb2_b = sb("rb2_b", [P, H])
        rw1_sb = sb("rw1_sb", [P, CW1])
        rw2_sb = sb("rw2_sb", [P, KC, HALF])
        dist_sb = sb("dist_sb", [P, NBLOCK * TILES])
        cw_a = sb("cw_a", [P, NBLOCK * TILES])
        cw_b = sb("cw_b", [P, NBLOCK * TILES])
        cw_all = sb("cw_all", [P, NBLOCK * TILES])

        idx = pair_of(sb, "idx", [P, 2 * TILES], I32)
        rows = pair_of(sb, "rows", [P, BE], I32)
        feat = pair_of(sb, "feat", [RAD, BE])
        nodes = pair_of(sb, "nodes", [P, G1, TW])
        once = pair_of(sb, "once", [P, TILES], I32)
        kept_out = pair_of(sb, "kept_out", [P, G2 + TILES, H])
        sums = pair_of(sb, "sums", [P, TILES, AW])
        stats = sb("stats", [P, G1, 6])
        mean2 = sb("mean2", [P, G1])
        mdiff = sb("mdiff", [P, G1])
        vsum = sb("vsum", [P, G1])
        vmix = sb("vmix", [P, G1])
        var = sb("var", [P, G1])
        std = sb("std", [P, G1])
        rstd = pair_of(sb, "rstd", [P, G1])
        shift = pair_of(sb, "shift", [P, G1])
        hid = pair_of(sb, "hid", [P, G2, H])
        zdst = sb("zdst", [P, TILES, H])
        hsum = pair_of(sb, "hsum", [P, G2])
        hmean = sb("hmean", [P, G2])
        same_a = pair_of(sb, "same_a", [P, 2, P])
        same_b = pair_of(sb, "same_b", [P, 2, 2 * P])
        junk = sb("junk", [P, TILES, 2 * P])
        junk_q = sb("junk_q", [P, TILES, NTYPE])
        ahead = sb("ahead", [P, TILES])
        turn = sb("turn", [P, TILES])
        turned = sb("turned", [P, TILES])
        onehot = sb("onehot", [P, TILES, NTYPE])
        onehot_t = sb("onehot_t", [NTYPE, TILES, P])
        gate_in = pair_of(sb, "gate_in", [P, BE // 2])
        logit = sb("logit", [P, TILES])
        coef = sb("coef", [P, TILES])
        hdst = sb("hdst", [P, TILES, H])
        msg_raw = sb("msg_raw", [P, TILES, H])
        msum = sb("msum", [P, TILES])
        mmean = sb("mmean", [P, TILES])
        msg = sb("msg", [P, TILES, AW])
        agg_in = pair_of(sb, "agg_in", [P, G2, AW])
        kept_in = pair_of(sb, "kept_in", [P, G2 + TILES, H])
        chunk_x = pair_of(sb, "chunk_x", [P, NR, TW])
        norm_all = sb("norm_all", [P, NBLOCK * TILES])
        rel_all = sb("rel_all", [P, NBLOCK * TILES], I32)
        dkey = pair_of(sb, "dkey", [P, TILES], I32)
        once1 = pair_of(sb, "once1", [P, TILES], I32)
        stat = sb("stat", [P, TILES])
        nmean = sb("nmean", [P, TILES])
        cen = sb("cen", [P, TILES, H])
        sq = sb("sq", [P, TILES, H])
        evar = sb("evar", [P, TILES])
        estd = sb("estd", [P, TILES])
        erstd = sb("erstd", [P, TILES])
        junk1 = sb("junk1", [P, TILES, 2 * P])
        ahead1 = sb("ahead1", [P, TILES])
        turn1 = sb("turn1", [P, TILES])
        turned1 = sb("turned1", [P, TILES])
        x2 = pair_of(sb, "x2", [P, G2, H])
        sums1 = pair_of(sb, "sums1", [P, TILES, H])
        tot = sb("tot", [P, G2])
        rtot = sb("rtot", [P, G2])
        ycen = sb("ycen", [P, G2, H])
        ycen2 = sb("ycen2", [P, G2, H])
        ysq = sb("ysq", [P, G2, H])
        yvar = sb("yvar", [P, G2])
        ystd = sb("ystd", [P, G2])
        yrstd = sb("yrstd", [P, G2])
        ynrm = sb("ynrm", [P, G2, H])
        ygam = sb("ygam", [P, G2, H])
        h2 = sb("h2", [P, TILES, HALF])
        h2n = sb("h2n", [P, TILES, H])
        h2_t = sb("h2_t", [P, BE // 2])
        hid1 = sb("hid1", [P, KC, 2, BE // 2])
        msg1_t = sb("msg1_t", [P, BE // 2])
        msg1 = pair_of(sb, "msg1", [P, TILES, H])
        agg_last = slots_of(sb, "agg_last", [P, NR * H])
        x_beta = pair_of(sb, "x_beta", [P, NR, H])
        x_last = slots_of(sb, "x_last", [P, NR * H])
        out_sb = slots_of(sb, "out_sb", [P, NR * H])

        def psum(name, shape):
            return ctx.enter_context(nc.psum_tensor(name, shape, F32))

        ps_t = psum("ps_t", [P, 512])
        ps_q = psum("ps_q", [P, 512])
        ps_m = psum("ps_m", [P, 512])
        ps_s = psum("ps_s", [P, 512])
        ps_k = pair_of(psum, "ps_k", [P, 2, 512])

        consts_in = sem("consts_in")
        rw1_in = sem("rw1_in")
        rb1_in = sem("rb1_in")
        agg0_set = [sem(f"agg0_set_{k}") for k in range(ZERO_SLOTS)]
        agg1_set = sem("agg1_set")
        idx_in = pair_of(sem, "idx_in")
        feat_in = pair_of(sem, "feat_in")
        rows_in = pair_of(sem, "rows_in")
        chunk_in = pair_of(sem, "chunk_in")
        ends_in = pair_of(sem, "ends_in")
        added0 = pair_of(sem, "added0")
        kept_stored = pair_of(sem, "kept_stored")
        names1 = ("stats_done mean2_done mdiff_done vsum_done vmix_done var_done std_done rstd_done shift_done "
                  "zdst_done hid_ends_done hid_done "
                  "hmean_done kept_done ahead_done turn_done turned_done once_done same_done "
                  "onehot_done onehot_t_done onehot_copied q_done logit_done h1_done gate_in_done gate_done "
                  "coef_done hdst_done raw_done mmean_done msg_done sums_done sums_copied").split()
        names2 = ("tot_done rtot_done ydiv_done ycen_done ysq_done yvar_done ystd_done yrstd_done ynrm_done "
                  "ygam_done x2_done esum_done emean_done ecen_done esq_done evar_done estd_done erstd_done "
                  "enrm_done h2_done rel_done h2t_done h2t_copied k0_done k1_done k2_done relu0_done relu1_done relu2_done "
                  "m1_done m1_copied m1t_done msg1_done same1_done ahead1_done turn1_done turned1_done once1_done "
                  "sums1_done sums1_copied").split()
        S = {n: sem(n) for n in names1 + names2}
        agg_chunk_in = pair_of(sem, "agg_chunk_in")
        agg_ends_in = pair_of(sem, "agg_ends_in")
        kept_got = pair_of(sem, "kept_got")
        idx2_in = pair_of(sem, "idx2_in")
        rows2_in = pair_of(sem, "rows2_in")
        adds0_done = sem("adds0_done")
        adds1_done = sem("adds1_done")
        added1 = pair_of(sem, "added1")
        x_stored = pair_of(sem, "x_stored")
        last_in = slots_of(sem, "last_in")
        out_done = sem("out_done")
        x_beta_done = sem("x_beta_done")
        out_stored = slots_of(sem, "out_stored")
        pool_set = sem("pool_set")
        vec_set = sem("vec_set")
        act_set = sem("act_set")
        pe_set = sem("pe_set")
        sp_steps = sem("sp_steps")
        pool_steps = sem("pool_steps")
        act_steps = sem("act_steps")
        pe_steps = sem("pe_steps")

        def hold(eng, steps, semaphore, value):
            eng.wait_ge(semaphore, value)
            eng.sem_inc(steps, 1)

        def ready(b):
            return b + 3

        def free1(b):
            return b + 2

        def free2(b):
            return b + 1

        def run(eng, block_body):
            with eng.Fori(0, ROUNDS) as i:
                for s in range(SLOTS):
                    block_body(i, s)
            block_body(ROUNDS, 0)

        def skewed(eng, turn):
            turn(0, 0, True, False, False, False)
            turn(0, 1, True, True, False, False)
            turn(1, 0, True, True, True, False)
            turn(1, 1, True, True, True, True)
            with eng.Fori(2, LOOPS) as i:
                turn(i, 0, True, True, True, True)
                turn(i, 1, True, True, True, True)
            turn(LOOPS, 0, True, True, True, True)
            turn(LOOPS, 1, False, True, True, True)
            turn(LOOPS + 1, 0, False, False, True, True)
            turn(LOOPS + 1, 1, False, False, False, True)

        def last_of(k):
            return max(c for c in range(KC) if c % 2 == k % 2)

        def chunk_rows(k):
            return ps_k[k % 2][:, :, 0:BE // 2]

        ps_hidden = [ps_k[1][:, 0, :], ps_k[0][:, 1, :]]

        def gate_rows(t):
            return (ps_m[:, :], ps_k[0][:, 0, :])[t // 2][:, t % 2 * H:(t % 2 + 1) * H]

        blk = ctx.enter_context(nc.Block())

        @blk.sync
        def _(sp):
            def bc(a, n):
                return a.rearrange("(o n) -> o n", o=1).to_broadcast([P, n])

            def flat(a):
                return a.rearrange("o p w -> (o p) w")

            def zero_chunk(r, k, again):
                if again:
                    hold(sp, sp_steps, agg0_set[k], r * 16)
                sp.dma_start(flat(agg0_chunks[bass.ds(r * ZERO_SLOTS + k, 1)]), zeros[:, :]).then_inc(agg0_set[k], 16)

            def zero_rounds(first, last):
                with sp.Fori(first, last) as r:
                    for k in range(ZERO_SLOTS):
                        zero_chunk(r, k, True)

            def stage1_early(i, s):
                b = i * 2 + s
                hold(sp, sp_steps, S["h1_done"], free2(b))
                sp.dma_start(feat[s][:, :], edge_feat[bass.ds(b, 1)].rearrange("o f e -> (o f) e")).then_inc(feat_in[s], 16)
                hold(sp, sp_steps, S["stats_done"], free2(b))
                hold(sp, sp_steps, S["same_done"], free2(b))
                hold(sp, sp_steps, S["once_done"], free2(b))
                sp.dma_start(idx[s][:, :], flat(edge_idx[bass.ds(b, 1)])).then_inc(idx_in[s], 16)
                sp.dma_start(rows[s][:, :], edge_rows[bass.ds(b, 1), BE:2 * BE].to_broadcast([P, BE])).then_inc(rows_in[s], 16)

            def stage1_late(i, s):
                b = i * 2 + s
                hold(sp, sp_steps, S["msg_done"], free2(b))
                hold(sp, sp_steps, S["hid_done"], free2(b))
                sp.dma_start(nodes[s][:, 2 * TILES:G1, :].rearrange("p r w -> p (r w)"),
                             flat(table_chunks[bass.ds(b, 1)])).then_inc(chunk_in[s], 16)

            def stage1_store(i, s):
                b = i * 2 + s
                sp.dma_start(flat(agg1_chunks[bass.ds(b, 1)]), bias_rows[:, :, :].rearrange("p r w -> p (r w)")).then_inc(agg1_set, 16)
                hold(sp, sp_steps, S["kept_done"], ready(b))
                sp.dma_start(flat(kept[bass.ds(b, 1)]), kept_out[s][:, :, :].rearrange("p r w -> p (r w)")).then_inc(kept_stored[s], 16)

            for s in range(2):
                stage1_early(0, s)
                stage1_late(0, s)
            sp.wait_ge(pool_set, 1)
            for k in range(ZERO_SLOTS):
                zero_chunk(0, k, False)
            sp.dma_start(adaptt_sb[:, :], adaptt).then_inc(consts_in, 16)
            sp.dma_start(embt_sb[:, :], embt).then_inc(consts_in, 16)
            sp.dma_start(dist_sb[:, :], dist).then_inc(consts_in, 16)
            sp.dma_start(w1t_sb[:, :], w1t).then_inc(consts_in, 16)
            for h in (0, HALF):
                sp.dma_start(b1_sb[h:h + H, :], b1.rearrange("(n o) -> n o", o=1)).then_inc(consts_in, 16)
                sp.dma_start(w2b_sb[h:h + H + 1, :], w2b).then_inc(consts_in, 16)
            sp.dma_start(gamma_b[:, :], bc(gamma, H)).then_inc(consts_in, 16)
            sp.dma_start(beta_b[:, :], bc(beta, H)).then_inc(consts_in, 16)
            sp.dma_start(rb2_b[:, :], bc(rb2, H)).then_inc(consts_in, 16)
            sp.dma_start(norm_all[:, :], norm).then_inc(consts_in, 16)
            sp.dma_start(rel_all[:, :], rel).then_inc(consts_in, 16)
            zero_rounds(1, ZERO_1)
            stage1_early(1, 0)
            zero_rounds(ZERO_1, ZERO_2)
            stage1_late(1, 0)
            stage1_early(1, 1)
            zero_rounds(ZERO_2, ZERO_ROUNDS)
            for k in range(NBLOCK - ZERO_ROUNDS * ZERO_SLOTS):
                zero_chunk(ZERO_ROUNDS, k, True)
            sp.wait_ge(pool_set, 13)
            for h in (0, HALF):
                sp.dma_start(rw1_sb[h:h + H, :], rw1).then_inc(rw1_in, 16)
            sp.dma_start(rw2_sb[:, :, 0:H], rw2.rearrange("(k p) h -> p k h", p=P)).then_inc(rw1_in, 16)
            for r in range(NREL):
                for h in (0, HALF):
                    sp.dma_start(rw1_sb[h + H + r:h + H + r + 1, r * H:(r + 1) * H], rb1.rearrange("(o n) -> o n", o=1)).then_inc(rb1_in, 16)
            sp.wait_ge(vec_set, 3)
            stage1_store(0, 0)
            stage1_late(1, 1)
            with sp.Fori(2, LOOPS) as i:
                stage1_early(i, 0)
                stage1_store(i - 2, 1)
                stage1_late(i, 0)
                stage1_early(i, 1)
                stage1_store(i - 1, 0)
                stage1_late(i, 1)
            stage1_early(LOOPS, 0)
            stage1_store(LOOPS - 2, 1)
            stage1_late(LOOPS, 0)
            stage1_store(LOOPS - 1, 0)
            stage1_store(LOOPS - 1, 1)
            stage1_store(LOOPS, 0)

            sp.wait_ge(kept_stored[0], 16 * (LOOPS + 1))
            sp.wait_ge(kept_stored[1], 16 * LOOPS)
            sp.wait_ge(added0[0], ADDS * (LOOPS + 1))
            sp.wait_ge(added0[1], ADDS * LOOPS)

            def stage2_idx(i, s):
                b = i * 2 + s
                hold(sp, sp_steps, S["tot_done"], free2(b))
                sp.dma_start(idx[s][:, :], flat(edge_idx[bass.ds(b, 1)])).then_inc(idx2_in[s], 16)

            def stage2_rows(i, s):
                b = i * 2 + s
                hold(sp, sp_steps, S["same1_done"], free2(b))
                hold(sp, sp_steps, S["once1_done"], free2(b))
                sp.dma_start(rows[s][:, :], edge_rows[bass.ds(b, 1), 0:BE].to_broadcast([P, BE])).then_inc(rows2_in[s], 16)
                sp.dma_start(dkey[s][:, :], flat(edge_idx[bass.ds(b, 1), :, 0:TILES])).then_inc(rows2_in[s], 16)

            def stage2_chunk(i, s, first):
                b = i * 2 + s
                hold(sp, sp_steps, S["x2_done"], free2(b))
                if not first:
                    hold(sp, sp_steps, x_stored[s], i * 16)
                sp.dma_start(agg_in[s][:, TILES:G2, :].rearrange("p r w -> p (r w)"),
                             flat(agg0_chunks[bass.ds(b, 1)])).then_inc(agg_chunk_in[s], 16)
                sp.dma_start(kept_in[s][:, :, :].rearrange("p r w -> p (r w)"), flat(kept[bass.ds(b, 1)])).then_inc(kept_got[s], 16)
                sp.dma_start(chunk_x[s][:, :, :].rearrange("p r w -> p (r w)"), flat(table_chunks[bass.ds(b, 1)])).then_inc(kept_got[s], 16)

            def stage2_store(i, s):
                b = i * 2 + s
                hold(sp, sp_steps, S["x2_done"], ready(b))
                sp.dma_start(flat(x_mid[bass.ds(b, 1)]), x2[s][:, TILES:G2, :].rearrange("p r w -> p (r w)")).then_inc(x_stored[s], 16)

            for s in range(2):
                stage2_idx(0, s)
                stage2_chunk(0, s, True)
            with sp.Fori(0, LOOPS - 1) as i:
                for s in range(2):
                    stage2_idx(i + 1, s)
                    stage2_rows(i, s)
                    stage2_store(i, s)
                    stage2_chunk(i + 1, s, False)
            stage2_idx(LOOPS, 0)
            stage2_rows(LOOPS - 1, 0)
            stage2_store(LOOPS - 1, 0)
            stage2_chunk(LOOPS, 0, False)
            stage2_rows(LOOPS - 1, 1)
            stage2_store(LOOPS - 1, 1)
            stage2_rows(LOOPS, 0)
            stage2_store(LOOPS, 0)

            sp.wait_ge(x_stored[0], 16 * (LOOPS + 1))
            sp.wait_ge(x_stored[1], 16 * LOOPS)
            sp.wait_ge(added1[0], ADDS * (LOOPS + 1))
            sp.wait_ge(added1[1], ADDS * LOOPS)

            def stage3_loads(i, s, first):
                b = i * SLOTS + s
                if not first:
                    hold(sp, sp_steps, out_done, b - SLOTS + 3)
                    hold(sp, sp_steps, out_stored[s], i * 16)
                sp.dma_start(agg_last[s][:, :], flat(agg1_chunks[bass.ds(b, 1)])).then_inc(last_in[s], 16)
                sp.dma_start(x_last[s][:, :], flat(x_mid[bass.ds(b, 1)])).then_inc(last_in[s], 16)

            for s in range(SLOTS):
                stage3_loads(0, s, True)
            with sp.Fori(1, ROUNDS) as i:
                for s in range(SLOTS):
                    stage3_loads(i, s, False)
            stage3_loads(ROUNDS, 0, False)
            for s in range(SLOTS):
                sp.wait_ge(out_stored[s], 16 * (ROUNDS + (s == 0)))

        @blk.gpsimd
        def _(pool):
            nc.gpsimd.memset(zeros[:, :], 0.0).then_inc(pool_set, 1)
            nc.gpsimd.memset(ident[:, :], 0.0).then_inc(pool_set, 1)
            nc.gpsimd.memset(earlier[:, :], 1.0).then_inc(pool_set, 1)
            nc.gpsimd.memset(rw1_sb[:, :], OFF).then_inc(pool_set, 1)
            nc.gpsimd.memset(h2[:, :, :], 0.0).then_inc(pool_set, 1)
            nc.gpsimd.memset(gate_in[0][:, :], 1.0).then_inc(pool_set, 1)
            nc.gpsimd.memset(gate_in[1][:, :], 1.0).then_inc(pool_set, 1)
            nc.gpsimd.memset(rw2_sb[:, :, :], 0.0).then_inc(pool_set, 1)
            nc.gpsimd.memset(half_pi[:, :], float(np.pi / 2)).then_inc(pool_set, 1)
            nc.gpsimd.memset(eps[:, :], EPS).then_inc(pool_set, 1)
            nc.gpsimd.iota(iota_type[:, :], pattern=[[1, NTYPE]], base=0, channel_multiplier=0,
                           allow_small_or_imprecise_dtypes=True).then_inc(pool_set, 1)
            nc.gpsimd.iota(iota_rel[:, :], pattern=[[1, NREL]], base=0, channel_multiplier=0,
                           allow_small_or_imprecise_dtypes=True).then_inc(pool_set, 1)
            nc.gpsimd.iota(dump_id[:, :, :], pattern=[[0, TILES // 2], [P, 2]], base=DUMP, channel_multiplier=1,
                           allow_small_or_imprecise_dtypes=True).then_inc(pool_set, 1)
            pool.wait_ge(pool_set, 13)
            nc.gpsimd.affine_select(out=ident[:, :], in_=ident[:, :], compare_op=ALU.not_equal, fill=1.0, base=0,
                                    pattern=[[-1, P]], channel_multiplier=1).then_inc(pool_set, 1)
            nc.gpsimd.affine_select(out=earlier[:, P:2 * P], in_=earlier[:, P:2 * P], compare_op=ALU.is_gt, fill=0.0,
                                    base=0, pattern=[[-1, P]], channel_multiplier=1).then_inc(pool_set, 1)
            pool.sem_inc(adds0_done, 2)
            pool.sem_inc(adds1_done, 2)

            def was_added0(i, s):
                hold(pool, adds0_done, added0[s], (i + 1) * ADDS)

            def was_added1(i, s):
                hold(pool, adds1_done, added1[s], (i + 1) * ADDS)

            def gather_ends(i, s, half):
                b = i * 2 + s
                if half == 0:
                    hold(pool, pool_steps, idx_in[s], (i + 1) * 16)
                    hold(pool, pool_steps, S["hid_ends_done"], free2(b))
                    hold(pool, pool_steps, S["zdst_done"], free2(b))
                else:
                    hold(pool, pool_steps, S["msg_done"], free2(b))
                for t in range((1 - half) * TILES, (2 - half) * TILES):
                    pool.indirect_dma_start(nodes[s][:, t, :], None, table,
                                            bass.IndirectOffsetOnAxis(ap=idx[s][:, t:t + 1], axis=0)).then_inc(ends_in[s], 16)

            def add0(i, s, q):
                b = i * 2 + s
                if q == 0:
                    hold(pool, pool_steps, S["once_done"], ready(b))
                    hold(pool, pool_steps, S["sums_copied"], ready(b))
                else:
                    hold(pool, pool_steps, added0[s], i * ADDS + 32 * q)
                for t in (2 * q, 2 * q + 1):
                    pool.indirect_dma_start(agg0, bass.IndirectOffsetOnAxis(ap=once[s][:, t:t + 1], axis=0),
                                            sums[s][:, t, :], None, compute_op=ALU.add).then_inc(added0[s], 16)

            for s in range(2):
                gather_ends(0, s, 0)
                gather_ends(0, s, 1)
            gather_ends(1, 0, 0)
            gather_ends(1, 0, 1)
            gather_ends(1, 1, 0)
            for k in range(ZERO_SLOTS):
                pool.wait_ge(agg0_set[k], 16 * (ZERO_ROUNDS + (k < NBLOCK - ZERO_ROUNDS * ZERO_SLOTS)))
            add0(0, 0, 0)
            add0(0, 0, 1)
            def adds_and_gathers(i, more):
                was_added0(i - 1, 0)
                add0(i - 1, 1, 0)
                gather_ends(i, 1, 1)
                add0(i - 1, 1, 1)
                gather_ends(i + 1, 0, 0)
                was_added0(i - 1, 1)
                add0(i, 0, 0)
                gather_ends(i + 1, 0, 1)
                add0(i, 0, 1)
                if more:
                    gather_ends(i + 1, 1, 0)

            with pool.Fori(1, LOOPS - 1) as i:
                adds_and_gathers(i, True)
            adds_and_gathers(LOOPS - 1, False)
            was_added0(LOOPS - 1, 0)
            add0(LOOPS - 1, 1, 0)
            add0(LOOPS - 1, 1, 1)
            was_added0(LOOPS - 1, 1)
            add0(LOOPS, 0, 0)
            add0(LOOPS, 0, 1)
            pool.wait_ge(added0[0], ADDS * (LOOPS + 1))

            def gather_agg0(i, s):
                b = i * 2 + s
                hold(pool, pool_steps, idx2_in[s], (i + 1) * 16)
                hold(pool, pool_steps, S["ydiv_done"], free2(b))
                for t in range(TILES):
                    pool.indirect_dma_start(agg_in[s][:, t, :], None, agg0,
                                            bass.IndirectOffsetOnAxis(ap=idx[s][:, TILES + t:TILES + t + 1], axis=0)).then_inc(agg_ends_in[s], 16)

            def add1(i, s):
                b = i * 2 + s
                hold(pool, pool_steps, S["once1_done"], ready(b))
                hold(pool, pool_steps, S["sums1_copied"], ready(b))
                for q in range(TILES // 2):
                    if q:
                        hold(pool, pool_steps, added1[s], i * ADDS + 32 * q)
                    for t in (2 * q, 2 * q + 1):
                        pool.indirect_dma_start(agg1, bass.IndirectOffsetOnAxis(ap=once1[s][:, t:t + 1], axis=0),
                                                sums1[s][:, t, :], None, compute_op=ALU.add).then_inc(added1[s], 16)

            for i, s in ((0, 0), (0, 1), (1, 0), (1, 1), (2, 0)):
                gather_agg0(i, s)
            pool.wait_ge(agg1_set, 16 * NBLOCK)
            gather_agg0(2, 1)
            add1(0, 0)
            gather_agg0(3, 0)
            was_added1(0, 0)
            add1(0, 1)
            with pool.Fori(2, LOOPS - 1) as i:
                was_added1(i - 2, 1)
                gather_agg0(i + 1, 1)
                add1(i - 1, 0)
                was_added1(i - 1, 0)
                gather_agg0(i + 2, 0)
                add1(i - 1, 1)
            was_added1(LOOPS - 3, 1)
            add1(LOOPS - 2, 0)
            for i, s in ((LOOPS - 2, 1), (LOOPS - 1, 0), (LOOPS - 1, 1), (LOOPS, 0)):
                was_added1(*((i, 0) if s else (i - 1, 1)))
                add1(i, s)
            pool.wait_ge(added1[0], ADDS * (LOOPS + 1))

        @blk.tensor
        def _(pe):
            for n in ("onehot_t_done", "q_done", "h1_done", "gate_done", "sums_done",
                      "h2t_done", "k0_done", "k1_done", "k2_done", "m1_done", "m1t_done", "sums1_done"):
                pe.sem_inc(S[n], 2)
            pe.wait_ge(consts_in, CONSTS)
            nc.tensor.matmul(ps_t[0:GEMB, 0:NTYPE], adaptt_sb[:, :], embt_sb[:, :], start=True, stop=True).then_inc(pe_set, 1)
            pe.wait_ge(vec_set, 1)
            nc.tensor.matmul(ps_q[0:NTYPE, 0:NTYPE], embt_sb[:, :], ada[:, :], start=True, stop=True).then_inc(pe_set, 1)
            pe.wait_ge(pool_set, 15)
            pe.wait_ge(vec_set, 2)

            def h1(i, s):
                b = i * 2 + s
                hold(pe, pe_steps, feat_in[s], (i + 1) * 16)
                hold(pe, pe_steps, S["gate_in_done"], free2(b))
                for h in range(2):
                    last = nc.tensor.matmul(ps_hidden[s][HALF * h:HALF * h + H, 0:BE // 2], w1t_sb[:, :],
                                            feat[s][:, h * (BE // 2):(h + 1) * (BE // 2)], start=True, stop=True)
                last.then_inc(S["h1_done"], 1)

            def sums_of_pairs(s, width, m):
                for q in range(TILES // 2):
                    a = 2 * q
                    nc.tensor.matmul(ps_s[:, a * width:(a + 1) * width], same_a[s][:, q, :], m[:, a, :], start=True, stop=False)
                    nc.tensor.matmul(ps_s[:, a * width:(a + 1) * width], same_b[s][:, q, 0:P], m[:, a + 1, :], start=False, stop=True)
                    last = nc.tensor.matmul(ps_s[:, (a + 1) * width:(a + 2) * width], same_b[s][:, q, P:2 * P], m[:, a + 1, :],
                                            start=True, stop=True)
                return last

            def stage1(i, s):
                b = i * 2 + s
                hold(pe, pe_steps, S["onehot_done"], ready(b))
                hold(pe, pe_steps, S["onehot_copied"], free1(b))
                for t in range(TILES):
                    last = nc.tensor.transpose(ps_t[0:NTYPE, t * P:(t + 1) * P], onehot[:, t, :], ident[:, :])
                last.then_inc(S["onehot_t_done"], 1)
                hold(pe, pe_steps, S["onehot_copied"], ready(b))
                hold(pe, pe_steps, S["logit_done"], free1(b))
                for t in range(TILES):
                    last = nc.tensor.matmul(ps_q[:, t * NTYPE:(t + 1) * NTYPE], onehot_t[:, t, :], q_sb[:, :], start=True, stop=True)
                last.then_inc(S["q_done"], 1)
                hold(pe, pe_steps, S["gate_in_done"], ready(b))
                hold(pe, pe_steps, S["msg_done"], free1(b))
                for t in range(TILES):
                    h = HALF * (t // 2)
                    last = nc.tensor.matmul(gate_rows(t), gate_in[s][h:h + H + 1, t % 2 * P:(t % 2 + 1) * P],
                                            w2b_sb[h:h + H + 1, :], start=True, stop=True)
                last.then_inc(S["gate_done"], 1)
                hold(pe, pe_steps, S["same_done"], ready(b))
                hold(pe, pe_steps, S["msg_done"], ready(b))
                hold(pe, pe_steps, S["sums_copied"], free1(b))
                sums_of_pairs(s, AW, msg).then_inc(S["sums_done"], 1)

            h1(0, 0)
            h1(0, 1)
            with pe.Fori(0, LOOPS - 1) as i:
                stage1(i, 0)
                stage1(i, 1)
                h1(i + 1, 0)
                h1(i + 1, 1)
            stage1(LOOPS - 1, 0)
            stage1(LOOPS - 1, 1)
            h1(LOOPS, 0)
            stage1(LOOPS, 0)
            pe.wait_ge(rw1_in, 3 * 16)
            pe.wait_ge(rb1_in, 2 * 16 * NREL)

            def stage2(i, s, y, e, d, f):
                b = i * 2 + s
                if e:
                    hold(pe, pe_steps, S["rel_done"], ready(b - 1))
                    hold(pe, pe_steps, S["h2_done"], ready(b - 1))
                    hold(pe, pe_steps, S["h2t_copied"], free1(b - 1))
                    for q in range(TILES // 2):
                        last = nc.tensor.transpose(ps_t[:, q * P:(q + 1) * P], h2[:, 2 * q:2 * q + 2, :].rearrange("p t w -> p (t w)"), ident[:, :])
                    last.then_inc(S["h2t_done"], 1)
                if d:
                    hold(pe, pe_steps, S["m1_copied"], ready(b - 2))
                    hold(pe, pe_steps, S["msg1_done"], free1(b - 2))
                    for t in range(TILES // 2):
                        last = nc.tensor.transpose(ps_q[:, t * P:(t + 1) * P], msg1_t[:, t * P:(t + 1) * P], ident[:, :])
                    last.then_inc(S["m1t_done"], 1)
                if f:
                    hold(pe, pe_steps, S["same1_done"], ready(b - 3))
                    hold(pe, pe_steps, S["msg1_done"], ready(b - 3))
                    hold(pe, pe_steps, S["sums1_copied"], free1(b - 3))
                    sums_of_pairs(1 - s, H, msg1[1 - s]).then_inc(S["sums1_done"], 1)
                if e:
                    hold(pe, pe_steps, S["h2t_copied"], ready(b - 1))
                    for k in range(KC):
                        if k < 2:
                            hold(pe, pe_steps, S[f"relu{last_of(k)}_done"], free1(b - 1))
                        else:
                            hold(pe, pe_steps, S[f"relu{k - 2}_done"], ready(b - 1))
                        for h in range(2):
                            last = nc.tensor.matmul(chunk_rows(k)[:, h, :], rw1_sb[HALF * h:HALF * h + H + NREL, k * P:(k + 1) * P],
                                                    h2_t[HALF * h:HALF * h + H + NREL, :], start=True, stop=True)
                        last.then_inc(S[f"k{k}_done"], 1)
                if e:
                    hold(pe, pe_steps, S["m1_copied"], free1(b - 1))
                    for k in range(KC):
                        hold(pe, pe_steps, S[f"relu{k}_done"], ready(b - 1))
                        for h in range(2):
                            last = nc.tensor.matmul(ps_m[HALF * h:HALF * (h + 1), 0:BE // 2], rw2_sb[:, k, :],
                                                    hid1[:, k, h, :], start=(k == 0), stop=(k == KC - 1))
                    last.then_inc(S["m1_done"], 1)

            skewed(pe, stage2)

        @blk.scalar
        def _(act):
            for n in ("onehot_copied", "gate_in_done", "std_done", "hid_ends_done", "hid_done", "sums_copied", "ysq_done",
                      "ystd_done", "esq_done", "estd_done", "h2_done", "h2t_copied", "relu0_done", "relu1_done",
                      "relu2_done", "m1_copied", "sums1_copied"):
                act.sem_inc(S[n], 2)
            act.wait_ge(pool_set, 13)
            act.wait_ge(vec_set, 4)
            nc.scalar.activation(cw_b[:, :], cw_a[:, :], ACT.Sin, bias=half_pi[:, :], scale=-float(np.pi) / CUTOFF).then_inc(act_set, 1)

            def gate_hidden(i, s):
                b = i * 2 + s
                hold(act, act_steps, S["h1_done"], ready(b))
                hold(act, act_steps, S["gate_done"], free2(b))
                for h in (0, HALF):
                    last = nc.scalar.activation(gate_in[s][h:h + H, :], ps_hidden[s][h:h + H, 0:BE // 2], ACT.Silu,
                                                bias=b1_sb[h:h + H, :], scale=1.0)
                last.then_inc(S["gate_in_done"], 1)

            def turned_and_std(i, s):
                b = i * 2 + s
                hold(act, act_steps, S["onehot_t_done"], ready(b))
                hold(act, act_steps, S["q_done"], free1(b))
                nc.scalar.copy(onehot_t[:, :, :].rearrange("p t e -> p (t e)"), ps_t[0:NTYPE, :]).then_inc(S["onehot_copied"], 1)
                hold(act, act_steps, S["var_done"], ready(b))
                hold(act, act_steps, S["rstd_done"], free1(b))
                nc.scalar.activation(std[:, :], var[:, :], ACT.Sqrt, bias=eps[:, :], scale=1.0 / H).then_inc(S["std_done"], 1)

            def hidden_and_sums(i, s):
                b = i * 2 + s
                hold(act, act_steps, S["kept_done"], free2(b))
                hold(act, act_steps, S["shift_done"], ready(b))
                for r in range(G2):
                    at = r + TILES
                    row = nc.scalar.activation(hid[s][:, r, :], nodes[s][:, at, 0:H], ACT.Relu, bias=shift[s][:, at:at + 1],
                                               scale=rstd[s][:, at:at + 1], accum_out=hsum[s][:, r:r + 1])
                    if r == TILES - 1:
                        row.then_inc(S["hid_ends_done"], 1)
                    if r == G2 - 1 - TILES:
                        hold(act, act_steps, adds0_done, free2(b))
                        hold(act, act_steps, S["sums_done"], ready(b))
                        nc.scalar.copy(sums[s][:, :, :].rearrange("p t w -> p (t w)"), ps_s[:, 0:TILES * AW]).then_inc(S["sums_copied"], 1)
                row.then_inc(S["hid_done"], 1)

            act.wait_ge(consts_in, CONSTS)
            turned_and_std(0, 0)
            with act.Fori(0, LOOPS) as i:
                gate_hidden(i, 0)
                gate_hidden(i, 1)
                hidden_and_sums(i, 0)
                turned_and_std(i, 1)
                hidden_and_sums(i, 1)
                turned_and_std(i + 1, 0)
            gate_hidden(LOOPS, 0)
            hidden_and_sums(LOOPS, 0)

            def stage2(i, s, y, e, d, f):
                b = i * 2 + s
                if e:
                    hold(act, act_steps, S["ecen_done"], ready(b - 1))
                    hold(act, act_steps, S["evar_done"], free1(b - 1))
                    nc.scalar.activation(sq[:, :, :], cen[:, :, :], ACT.Square).then_inc(S["esq_done"], 1)
                if y:
                    hold(act, act_steps, S["ycen_done"], ready(b))
                    hold(act, act_steps, S["yvar_done"], free1(b))
                    nc.scalar.activation(ysq[:, :, :], ycen2[:, :, :], ACT.Square).then_inc(S["ysq_done"], 1)
                if d:
                    hold(act, act_steps, S[f"k{KC - 1}_done"], ready(b - 2))
                    nc.scalar.activation(hid1[:, KC - 1, :, :], chunk_rows(KC - 1), ACT.Relu).then_inc(S[f"relu{KC - 1}_done"], 1)
                if e:
                    hold(act, act_steps, S["evar_done"], ready(b - 1))
                    hold(act, act_steps, S["erstd_done"], free1(b - 1))
                    nc.scalar.activation(estd[:, :], evar[:, :], ACT.Sqrt, bias=eps[:, :], scale=1.0 / H).then_inc(S["estd_done"], 1)
                if y:
                    hold(act, act_steps, S["yvar_done"], ready(b))
                    hold(act, act_steps, S["yrstd_done"], free1(b))
                    nc.scalar.activation(ystd[:, :], yvar[:, :], ACT.Sqrt, bias=eps[:, :], scale=1.0 / H).then_inc(S["ystd_done"], 1)
                if d:
                    hold(act, act_steps, S["m1_done"], ready(b - 2))
                    hold(act, act_steps, S["m1t_done"], free1(b - 2))
                    nc.scalar.copy(msg1_t[:, :], ps_m[:, 0:BE // 2]).then_inc(S["m1_copied"], 1)
                if e:
                    hold(act, act_steps, S["enrm_done"], ready(b - 1))
                    hold(act, act_steps, S["h2t_done"], free1(b - 1))
                    nc.scalar.activation(h2[:, :, 0:H], h2n[:, :, :], ACT.Relu).then_inc(S["h2_done"], 1)
                    hold(act, act_steps, S["h2t_done"], ready(b - 1))
                    hold(act, act_steps, S["k2_done"], free1(b - 1))
                    nc.scalar.copy(h2_t[:, :], ps_t[:, 0:BE // 2]).then_inc(S["h2t_copied"], 1)
                if f:
                    hold(act, act_steps, adds1_done, free2(b - 3))
                    hold(act, act_steps, S["sums1_done"], ready(b - 3))
                    nc.scalar.copy(sums1[1 - s][:, :, :].rearrange("p t w -> p (t w)"), ps_s[:, 0:TILES * H]).then_inc(S["sums1_copied"], 1)
                if e:
                    hold(act, act_steps, S["m1_done"], free1(b - 1))
                    for k in range(KC - 1):
                        hold(act, act_steps, S[f"k{k}_done"], ready(b - 1))
                        nc.scalar.activation(hid1[:, k, :, :], chunk_rows(k), ACT.Relu).then_inc(S[f"relu{k}_done"], 1)

            skewed(act, stage2)

            def stage3(i, s):
                b = i * SLOTS + s
                hold(act, act_steps, out_done, ready(b))
                act.dma_start(out_chunks[bass.ds(b, 1)].rearrange("o p w -> (o p) w"), out_sb[s][:, :]).then_inc(out_stored[s], 16)

            run(act, stage3)

        @blk.vector
        def _(dve):
            for n in ("stats_done mean2_done mdiff_done vsum_done vmix_done var_done rstd_done shift_done zdst_done hmean_done kept_done "
                      "ahead_done turn_done turned_done once_done same_done onehot_done logit_done coef_done hdst_done "
                      "raw_done mmean_done msg_done tot_done rtot_done ydiv_done ycen_done yvar_done yrstd_done "
                      "ynrm_done ygam_done x2_done esum_done emean_done ecen_done evar_done erstd_done enrm_done "
                      "rel_done msg1_done same1_done ahead1_done turn1_done turned1_done once1_done").split():
                dve.sem_inc(S[n], 2)
            dve.sem_inc(out_done, 2)
            dve.sem_inc(x_beta_done, 2)

            V = nc.vector

            def cols(a, n):
                return a.unsqueeze(2).to_broadcast([P, a.shape[1], n])

            def each(a, n):
                return a.unsqueeze(1).to_broadcast([P, n, a.shape[1]])

            dve.wait_ge(consts_in, CONSTS)
            dve.wait_ge(pe_set, 1)
            V.tensor_copy(ada[:, :], ps_t[0:GEMB, 0:NTYPE]).then_inc(vec_set, 1)
            dve.wait_ge(pe_set, 2)
            V.tensor_copy(q_sb[:, :], ps_q[0:NTYPE, 0:NTYPE]).then_inc(vec_set, 1)
            V.tensor_copy(bias_rows[:, :, :], each(rb2_b[:, :], NR)).then_inc(vec_set, 1)
            V.tensor_scalar(cw_all[:, :], dist_sb[:, :], -1.0, CUTOFF, ALU.mult, ALU.min).then_inc(act_set, 1)
            V.tensor_scalar(cw_b[:, :], dist_sb[:, :], CUTOFF, None, ALU.min).then_inc(act_set, 1)
            dve.wait_ge(act_set, 2)
            V.tensor_tensor(cw_a[:, :], cw_all[:, :], cw_b[:, :], ALU.max).then_inc(vec_set, 1)
            dve.wait_ge(act_set, 3)
            V.tensor_scalar(cw_a[:, :], cw_b[:, :], 1.0, 0.5, ALU.add, ALU.mult).then_inc(act_set, 1)
            dve.wait_ge(act_set, 4)
            V.scalar_tensor_tensor(out=cw_all[:, :], in0=dist_sb[:, :], scalar=CUTOFF, in1=cw_a[:, :],
                                   op0=ALU.is_lt, op1=ALU.mult).then_inc(act_set, 1)
            dve.wait_ge(act_set, 5)
            dve.wait_ge(pool_set, 15)

            def same_node(s, keys):
                for q in range(TILES // 2):
                    a = 2 * q
                    V.tensor_scalar(same_a[s][:, q, :], rows[s][:, a * P:(a + 1) * P], keys[:, a:a + 1], None, ALU.is_equal)
                    last = V.tensor_scalar(same_b[s][:, q, :], rows[s][:, a * P:(a + 2) * P],
                                           keys[:, a + 1:a + 2], None, ALU.is_equal)
                return last

            def count_ahead(s, keys, work, counts):
                for t in range(TILES):
                    a = t - t % 2
                    n = P * (1 + t % 2)
                    last = V.scalar_tensor_tensor(out=work[:, t, 0:n], in0=rows[s][:, a * P:a * P + n], scalar=keys[:, t:t + 1],
                                                  in1=earlier[:, 2 * P - n:2 * P], op0=ALU.is_equal, op1=ALU.mult,
                                                  accum_out=counts[:, t:t + 1])
                return last

            dump = dump_id[:, :, :].rearrange("p q a -> p (q a)")

            def keep_hidden(i, s):
                b = i * 2 + s
                dve.wait_ge(S["hid_done"], ready(b))
                V.tensor_scalar(hmean[:, :], hsum[s][:, :], -1.0 / H, None, ALU.mult).then_inc(S["hmean_done"], 1)
                dve.wait_ge(S["hmean_done"], ready(b))
                V.tensor_tensor(kept_out[s][:, 0:G2, :], hid[s][:, :, :], cols(hmean[:, :], H), ALU.add).then_inc(S["kept_done"], 1)

            def stage1(i, s, behind, first):
                b = i * 2 + s
                keys = idx[s][:, TILES:2 * TILES]
                dve.wait_ge(ends_in[s], (i + 1) * (2 * TILES * 16))
                dve.wait_ge(chunk_in[s], (i + 1) * 16)
                dve.wait_ge(S["onehot_t_done"], free1(b))
                V.tensor_tensor(onehot[:, :, :], each(iota_type[:, :], TILES),
                                nodes[s][:, TILES:2 * TILES, H + 1:H + 2].bitcast(I32).to_broadcast([P, TILES, NTYPE]),
                                ALU.is_equal).then_inc(S["onehot_done"], 1)
                for r in range(G1):
                    last = V.bn_stats(stats[:, r, :], nodes[s][:, r, 0:H])
                last.then_inc(S["stats_done"], 1)
                dve.wait_ge(S["stats_done"], ready(b))

                def of(n):
                    return stats[:, :, n:n + 1].rearrange("p r o -> p (r o)")

                V.tensor_tensor(mdiff[:, :], of(1), of(4), ALU.subtract).then_inc(S["mdiff_done"], 1)
                V.tensor_tensor(vsum[:, :], of(2), of(5), ALU.add).then_inc(S["vsum_done"], 1)
                V.tensor_tensor(mean2[:, :], of(1), of(4), ALU.add).then_inc(S["mean2_done"], 1)
                dve.wait_ge(S["mdiff_done"], ready(b))
                V.scalar_tensor_tensor(out=vmix[:, :], in0=mdiff[:, :], scalar=H / 4.0, in1=mdiff[:, :], op0=ALU.mult,
                                       op1=ALU.mult).then_inc(S["vmix_done"], 1)
                dve.wait_ge(rows_in[s], (i + 1) * 16)
                dve.wait_ge(idx_in[s], (i + 1) * 16)
                V.tensor_tensor(turn[:, :], dump, keys, ALU.subtract).then_inc(S["turn_done"], 1)
                dve.wait_ge(S["vmix_done"], ready(b))
                V.tensor_tensor(var[:, :], vsum[:, :], vmix[:, :], ALU.add).then_inc(S["var_done"], 1)
                count_ahead(s, keys, junk, ahead).then_inc(S["ahead_done"], 1)
                same_node(s, keys).then_inc(S["same_done"], 1)
                dve.wait_ge(S["ahead_done"], ready(b))
                V.scalar_tensor_tensor(out=turned[:, :], in0=ahead[:, :], scalar=0.0, in1=turn[:, :], op0=ALU.is_gt,
                                       op1=ALU.mult).then_inc(S["turned_done"], 1)
                node_w = nodes[s][:, 0:TILES, H:H + 1].rearrange("p t o -> p (t o)")
                V.tensor_tensor(coef[:, :], node_w, cw_all[:, bass.ds(b * TILES, TILES)], ALU.mult).then_inc(S["coef_done"], 1)
                dve.wait_ge(S["turned_done"], ready(b))
                dve.wait_ge(adds0_done, free2(b))
                V.tensor_tensor(once[s][:, :], keys, turned[:, :], ALU.add).then_inc(S["once_done"], 1)
                dve.wait_ge(S["std_done"], ready(b))
                V.reciprocal(rstd[s][:, :], std[:, :]).then_inc(S["rstd_done"], 1)
                dve.wait_ge(S["rstd_done"], ready(b))
                V.scalar_tensor_tensor(out=shift[s][:, :], in0=mean2[:, :], scalar=-0.5, in1=rstd[s][:, :], op0=ALU.mult,
                                       op1=ALU.mult).then_inc(S["shift_done"], 1)
                if not first:
                    dve.wait_ge(kept_stored[s], i * 16)
                V.tensor_tensor(kept_out[s][:, G2:G2 + TILES, :], nodes[s][:, TILES:2 * TILES, 0:H], each(beta_b[:, :], TILES), ALU.add)
                dve.wait_ge(S["shift_done"], ready(b))
                for t in range(TILES):
                    last = V.tensor_scalar(zdst[:, t, :], nodes[s][:, t, 0:H], rstd[s][:, t:t + 1], shift[s][:, t:t + 1],
                                           ALU.mult, ALU.add)
                last.then_inc(S["zdst_done"], 1)
                if behind:
                    keep_hidden(i + s - 1, 1 - s)
                dve.wait_ge(S["zdst_done"], ready(b))
                dve.wait_ge(S["coef_done"], ready(b))
                V.scalar_tensor_tensor(out=hdst[:, :, :], in0=zdst[:, :, :], scalar=0.0, in1=cols(coef[:, :], H), op0=ALU.max,
                                       op1=ALU.mult).then_inc(S["hdst_done"], 1)
                dve.wait_ge(S["q_done"], ready(b))
                for t in range(TILES):
                    last = V.scalar_tensor_tensor(out=junk_q[:, t, :], in0=iota_type[:, :],
                                                  scalar=nodes[s][:, t, H + 1:H + 2].bitcast(I32),
                                                  in1=ps_q[:, t * NTYPE:(t + 1) * NTYPE], op0=ALU.is_equal, op1=ALU.mult,
                                                  accum_out=logit[:, t:t + 1])
                last.then_inc(S["logit_done"], 1)
                dve.wait_ge(S["logit_done"], ready(b))
                dve.wait_ge(S["hdst_done"], ready(b))
                dve.wait_ge(S["gate_done"], ready(b))
                for t in range(TILES):
                    last = V.scalar_tensor_tensor(out=msg_raw[:, t, :], in0=gate_rows(t), scalar=logit[:, t:t + 1],
                                                  in1=hdst[:, t, :], op0=ALU.add, op1=ALU.mult, accum_out=msum[:, t:t + 1])
                last.then_inc(S["raw_done"], 1)
                dve.wait_ge(S["raw_done"], ready(b))
                V.tensor_scalar(mmean[:, :], msum[:, :], -1.0 / H, None, ALU.mult).then_inc(S["mmean_done"], 1)
                dve.wait_ge(S["sums_done"], free1(b))
                V.tensor_copy(msg[:, :, H:AW], nodes[s][:, 0:TILES, H:H + 1])
                dve.wait_ge(S["mmean_done"], ready(b))
                V.tensor_tensor(msg[:, :, 0:H], msg_raw[:, :, :], cols(mmean[:, :], H), ALU.add).then_inc(S["msg_done"], 1)

            stage1(0, 0, False, True)
            stage1(0, 1, True, True)
            with dve.Fori(1, LOOPS) as i:
                stage1(i, 0, True, False)
                stage1(i, 1, True, False)
            stage1(LOOPS, 0, True, False)
            keep_hidden(LOOPS, 0)

            def stage2(i, s, y, e, d, f):
                b = i * 2 + s
                if y:
                    dve.wait_ge(agg_chunk_in[s], (i + 1) * 16)
                    dve.wait_ge(agg_ends_in[s], (i + 1) * (TILES * 16))
                    V.tensor_scalar(tot[:, :], agg_in[s][:, :, H:AW].rearrange("p r o -> p (r o)"), 1e-8, None, ALU.max).then_inc(S["tot_done"], 1)
                if e:
                    dve.wait_ge(S["x2_done"], ready(b - 1))
                    V.tensor_reduce(stat[:, :], x2[1 - s][:, 0:TILES, :], AX_X, ALU.add).then_inc(S["esum_done"], 1)
                if y:
                    dve.wait_ge(S["tot_done"], ready(b))
                    V.reciprocal(rtot[:, :], tot[:, :]).then_inc(S["rtot_done"], 1)
                if e:
                    dve.wait_ge(S["esum_done"], ready(b - 1))
                    V.tensor_scalar(nmean[:, :], stat[:, :], -1.0 / H, None, ALU.mult).then_inc(S["emean_done"], 1)
                if y:
                    dve.wait_ge(S["rtot_done"], ready(b))
                    V.tensor_tensor(ycen[:, :, :], agg_in[s][:, :, 0:H], cols(rtot[:, :], H), ALU.mult).then_inc(S["ydiv_done"], 1)
                if e:
                    dve.wait_ge(S["emean_done"], ready(b - 1))
                    V.tensor_tensor(cen[:, :, :], x2[1 - s][:, 0:TILES, :], cols(nmean[:, :], H), ALU.add).then_inc(S["ecen_done"], 1)
                    dve.wait_ge(S["h2t_done"], free1(b - 1))
                    V.tensor_tensor(h2[:, :, H:H + NREL], each(iota_rel[:, :], TILES),
                                    rel_all[:, bass.ds((b - 1) * TILES, TILES)].unsqueeze(2).to_broadcast([P, TILES, NREL]),
                                    ALU.is_equal).then_inc(S["rel_done"], 1)
                if y:
                    dve.wait_ge(S["ydiv_done"], ready(b))
                    dve.wait_ge(kept_got[s], (i + 1) * 32)
                    V.tensor_tensor(ycen2[:, :, :], ycen[:, :, :], kept_in[s][:, 0:G2, :], ALU.add).then_inc(S["ycen_done"], 1)
                if e:
                    dve.wait_ge(S["esq_done"], ready(b - 1))
                    V.tensor_reduce(evar[:, :], sq[:, :, :], AX_X, ALU.add).then_inc(S["evar_done"], 1)
                if d:
                    dve.wait_ge(rows2_in[s], i * 32)
                    V.tensor_tensor(turn1[:, :], dump, dkey[s][:, :], ALU.subtract).then_inc(S["turn1_done"], 1)
                    dve.wait_ge(S["sums1_done"], free2(b - 2))
                    same_node(s, dkey[s]).then_inc(S["same1_done"], 1)
                if y:
                    dve.wait_ge(S["ysq_done"], ready(b))
                    V.tensor_reduce(yvar[:, :], ysq[:, :, :], AX_X, ALU.add).then_inc(S["yvar_done"], 1)
                if e:
                    dve.wait_ge(S["estd_done"], ready(b - 1))
                    V.reciprocal(erstd[:, :], estd[:, :]).then_inc(S["erstd_done"], 1)
                    dve.wait_ge(S["erstd_done"], ready(b - 1))
                    V.tensor_tensor(h2n[:, :, :], cen[:, :, :], cols(erstd[:, :], H), ALU.mult).then_inc(S["enrm_done"], 1)
                if d:
                    count_ahead(s, dkey[s], junk1, ahead1).then_inc(S["ahead1_done"], 1)
                if y:
                    dve.wait_ge(S["ystd_done"], ready(b))
                    V.reciprocal(yrstd[:, :], ystd[:, :]).then_inc(S["yrstd_done"], 1)
                if d:
                    dve.wait_ge(S["ahead1_done"], ready(b - 2))
                    dve.wait_ge(S["turn1_done"], ready(b - 2))
                    V.scalar_tensor_tensor(out=turned1[:, :], in0=ahead1[:, :], scalar=0.0, in1=turn1[:, :], op0=ALU.is_gt,
                                           op1=ALU.mult).then_inc(S["turned1_done"], 1)
                if y:
                    dve.wait_ge(S["yrstd_done"], ready(b))
                    V.tensor_tensor(ynrm[:, :, :], ycen2[:, :, :], cols(yrstd[:, :], H), ALU.mult).then_inc(S["ynrm_done"], 1)
                if d:
                    dve.wait_ge(S["turned1_done"], ready(b - 2))
                    dve.wait_ge(adds1_done, free2(b - 2))
                    V.tensor_tensor(once1[s][:, :], dkey[s][:, :], turned1[:, :], ALU.add).then_inc(S["once1_done"], 1)
                    dve.wait_ge(S["m1t_done"], ready(b - 2))
                    dve.wait_ge(S["sums1_done"], free2(b - 2))
                    V.tensor_tensor(msg1[s][:, :, :], ps_q[:, 0:2 * P].rearrange("p (t h) -> p t h", t=TILES)[:, :, 0:H],
                                    cols(norm_all[:, bass.ds((b - 2) * TILES, TILES)], H), ALU.mult).then_inc(S["msg1_done"], 1)
                if y:
                    dve.wait_ge(S["ynrm_done"], ready(b))
                    V.tensor_tensor(ygam[:, :, :], ynrm[:, :, :], each(gamma_b[:, :], G2), ALU.mult).then_inc(S["ygam_done"], 1)
                    dve.wait_ge(S["ygam_done"], ready(b))
                    V.tensor_tensor(x2[s][:, 0:TILES, :], ygam[:, 0:TILES, :], kept_in[s][:, G2:G2 + TILES, :], ALU.add)
                    V.tensor_tensor(x2[s][:, TILES:G2, :], ygam[:, TILES:G2, :], chunk_x[s][:, :, 0:H], ALU.add).then_inc(S["x2_done"], 1)

            skewed(dve, stage2)

            def stage3(i, s):
                b = i * SLOTS + s
                dve.wait_ge(last_in[s], (i + 1) * 32)
                V.tensor_tensor(x_beta[s % 2][:, :, :], x_last[s][:, :].rearrange("p (r h) -> p r h", r=NR), each(beta_b[:, :], NR),
                                ALU.add).then_inc(x_beta_done, 1)
                dve.wait_ge(x_beta_done, ready(b))
                V.scalar_tensor_tensor(out=out_sb[s][:, :], in0=agg_last[s][:, :], scalar=0.0,
                                       in1=x_beta[s % 2][:, :, :].rearrange("p r h -> p (r h)"),
                                       op0=ALU.max, op1=ALU.add).then_inc(out_done, 1)

            run(dve, stage3)


def kernel(**inputs):
    import concourse.bacc as bacc
    from concourse.bass_utils import run_bass_kernel_spmd

    a = {k: np.asarray(v) for k, v in inputs.items()}
    ep = NBLOCK * BE

    def edges(v, fill=0):
        full = np.full((ep,), fill, v.dtype)
        full[:E] = v.reshape(-1)
        return full.reshape(NBLOCK, TILES, P)

    def columns(v):
        return v.transpose(0, 2, 1)

    src, dst = edges(a["src"], NULL), edges(a["dst"], NULL)
    table = np.zeros((NP, TW), np.float32)
    table[:N, :H] = a["x"]
    table[:N, H] = a["node_vec"]
    table[:N, H + 1] = a["node_type_119"].astype(np.int32).view(np.float32)
    feat = np.zeros((ep, RAD), np.float32)
    feat[:E] = a["edge_attr_40"]
    arrays = {
        "table": table,
        "edge_idx": np.concatenate([columns(dst), columns(src)], 2),
        "edge_rows": np.concatenate([dst.reshape(NBLOCK, BE), src.reshape(NBLOCK, BE)], 1),
        "edge_feat": feat.reshape(NBLOCK, BE, RAD).transpose(0, 2, 1),
        "dist": columns(edges(a["edge_weight"])).transpose(1, 0, 2).reshape(P, NBLOCK * TILES),
        "norm": columns(edges(a["edge_weight1"])).transpose(1, 0, 2).reshape(P, NBLOCK * TILES),
        "rel": columns(edges(a["edge_type_8"])).transpose(1, 0, 2).reshape(P, NBLOCK * TILES),
        "w1t": a["L0_gnn_W1"].T,
        "b1": a["L0_gnn_b1"],
        "w2b": np.concatenate([a["L0_gnn_W2"].T, a["L0_gnn_b2"][None]], 0),
        "embt": a["L0_gnn_emb"].T,
        "adaptt": a["L0_gnn_adaptW"].T,
        "gamma": a["L0_gnn_gamma"],
        "beta": a["L0_gnn_beta"],
        "rw1": a["L1_gnn_weight1"].transpose(1, 0, 2).reshape(H, CW1),
        "rb1": a["L1_gnn_bias1"],
        "rw2": a["L1_gnn_weight2"].reshape(CW1, H),
        "rb2": a["L1_gnn_bias2"],
    }
    nc = bacc.Bacc("TRN2", target_bir_lowering=False, num_devices=1)
    given, aps = {}, []
    for name, v in arrays.items():
        v = np.ascontiguousarray(v)
        given[f"in_{name}"] = v
        aps.append(nc.dram_tensor(f"in_{name}", v.shape, mybir.dt.from_np(v.dtype), kind="ExternalInput").ap())
    out = nc.dram_tensor("out_0", (NP, H), F32, kind="ExternalOutput").ap()
    build(nc, *aps, out)
    r = run_bass_kernel_spmd(nc, [given], core_ids=[0])
    return r.results[0]["out_0"][:N]
```
